# Optimizing a Trainium2 kernel written in Bass

```python
import numpy as np
import jax
import jax.numpy as jnp

def _softmax(x, axis=-1):
    return jax.nn.softmax(x, axis=axis)

def _gelu(x):
    return jax.nn.gelu(x, approximate=True)

def _silu(x):
    return jax.nn.silu(x)

def _sigmoid(x):
    return jax.nn.sigmoid(x)

def _layernorm(x, axis=-1, eps=1e-05):
    m = jnp.mean(x, axis=axis, keepdims=True)
    v = jnp.var(x, axis=axis, keepdims=True)
    return (x - m) / jnp.sqrt(v + eps)

def _scatter_add(tgt, idx, src, axis=0):
    return tgt.at[idx].add(src)

def _segment_sum(src, seg, n):
    return jax.ops.segment_sum(src, seg, n)
kernel_name = 'mk_gnn_resnorm_d1_gnn_r32_1f46d2'

def setup_inputs(seed: int=0):
    np.random.seed(seed)
    _w = jnp.asarray

    def _rec_inputs():
        import jax
        import jax.numpy as jnp
        _gk = jax.random.key(seed)
        x = -0.0003713 + 1 * jax.random.normal(jax.random.fold_in(_gk, 1), (50000, 128), jnp.float32)
        _s = jax.random.randint(jax.random.fold_in(_gk, 2), (25000,), 0, 50000, jnp.int32)
        _d = jax.random.randint(jax.random.fold_in(_gk, 3), (25000,), 0, 50000, jnp.int32)
        _loop = jnp.arange(50000, dtype=jnp.int32)
        src = jnp.concatenate([_s, _d, _loop])
        dst = jnp.concatenate([_d, _s, _loop])
        _o = jnp.argsort(dst, stable=True)
        src = src[_o]
        dst = dst[_o]
        return (x, src, dst)
    x, src, dst = _rec_inputs()

    def _L0_gnn_setup():
        import jax, jax.numpy as jnp
        import numpy as np
        NUM_NODES = 3125
        NUM_EDGES = 50000
        IN_DIM = 128
        OUT_DIM = 128
        key = jax.random.key(seed)
        k_x, k_e, k_ws, k_bs, k_wn, k_bn = jax.random.split(key, 6)
        bound = 1.0 / np.sqrt(IN_DIM)
        return {'x': jax.random.normal(k_x, (NUM_NODES, IN_DIM), dtype=jnp.float32), 'W_self': jax.random.uniform(k_ws, (OUT_DIM, IN_DIM), jnp.float32, -bound, bound), 'b_self': jax.random.uniform(k_bs, (OUT_DIM,), jnp.float32, -bound, bound), 'W_neigh': jax.random.uniform(k_wn, (OUT_DIM, IN_DIM), jnp.float32, -bound, bound), 'b_neigh': jax.random.uniform(k_bn, (OUT_DIM,), jnp.float32, -bound, bound), 'edge_index': jax.random.randint(k_e, (2, NUM_EDGES), 0, NUM_NODES, dtype=jnp.int64)}
    _L0_gnn_all = _L0_gnn_setup()
    _L0_gnn_in = {k: v for k, v in _L0_gnn_all.items() if k in ('W_self', 'b_self', 'W_neigh', 'b_neigh')}
    del _L0_gnn_all
    return {'x': x, 'src': src, 'dst': dst, 'L0_gnn_W_self': _L0_gnn_in['W_self'], 'L0_gnn_b_self': _L0_gnn_in['b_self'], 'L0_gnn_W_neigh': _L0_gnn_in['W_neigh'], 'L0_gnn_b_neigh': _L0_gnn_in['b_neigh']}

def reference(x, src, dst, L0_gnn_W_self, L0_gnn_b_self, L0_gnn_W_neigh, L0_gnn_b_neigh):
    import jax
    import jax.numpy as jnp

    def _L0_gnn_ref(x, W_self, b_self, W_neigh, b_neigh, edge_index):
        import jax, jax.numpy as jnp
        import numpy as np
        NUM_NODES = 3125
        NUM_EDGES = 50000
        IN_DIM = 128
        OUT_DIM = 128
        h_self = x @ W_self.T + b_self
        src, dst = (edge_index[0], edge_index[1])
        messages = x[src] @ W_neigh.T + b_neigh
        h_neigh = jax.ops.segment_sum(messages, dst, num_segments=x.shape[0])
        return jax.nn.relu(h_self + h_neigh)
    edge_index = jnp.stack([src, dst])
    x = _layernorm(x + _L0_gnn_ref(x, L0_gnn_W_self, L0_gnn_b_self, L0_gnn_W_neigh, L0_gnn_b_neigh, edge_index), axis=-1)
    return x

_drawn_inputs = setup_inputs


def setup_inputs(seed=0):
    import zlib

    import numpy as np

    out = dict(_drawn_inputs(seed))
    spreads = {}
    factors = {}
    for name, (base, spread) in spreads.items():
        noise = np.random.default_rng([zlib.crc32(name.encode()), seed]).standard_normal(out[name].shape)
        drawn = base * np.exp(spread * noise) if base else spread * noise
        out[name] = jnp.asarray(drawn.astype(out[name].dtype))
    for name, factor in factors.items():
        out[name] = (out[name] * factor).astype(out[name].dtype)
    return out
```

```python
import numpy as np

import concourse.bass as bass
from concourse import mybir
from contextlib import ExitStack

FP32 = mybir.dt.float32
BF16 = mybir.dt.bfloat16
INT32 = mybir.dt.int32
ALU = mybir.AluOpType
ACT = mybir.ActivationFunctionType
AXIS_X = mybir.AxisListType.X

P = 128
NODES, DIM, EDGES = 50000, 128, 100000
EPS = 1e-5

EDGE_ROWS = 125
EDGE_COLS = EDGES // EDGE_ROWS
BLOCK = 200
BLOCKS = EDGES // BLOCK
BLOCKS_PER_ROW = EDGE_COLS // BLOCK

TILES = -(-NODES // P)
LAST_ROWS = NODES - (TILES - 1) * P
PACKED = EDGES - NODES
CHUNKS = -(-PACKED // P)
COLUMNS = 4
SPREAD = -(-(CHUNKS + 1) // COLUMNS)
ENTRIES = SPREAD * COLUMNS

WINDOW = 320
SHIFT_BITS = 8
PAD = 400
NO_NODE = 65535

SPAN = 3
DRIFT = 8
RING = 48
STAGE = 16
GATHER_SEMS = 12
ROW = DIM + 4
TABLE = SPAN + 1

TRIO = 3
TRIOS = -(-TILES // TRIO)
DEEP = 4

LOOPED = ((CHUNKS - DRIFT - SPAN) // TRIO - 1) // DEEP * DEEP

GEN_EDGES = 125
GEN_STEPS = EDGES // GEN_EDGES
GEN_ROWS = 125
GEN_TILES = NODES // GEN_ROWS
ZERO_ROWS = 28
SUM_ROWS = 14 * P * ZERO_ROWS


def gnn_kernel(nc, x, src, dst, w_self, b_self, w_neigh, b_neigh, out):
    with ExitStack() as ctx:
        def sb(name, shape, dtype=FP32):
            return ctx.enter_context(nc.sbuf_tensor(name, shape, dtype))

        def sem(name):
            return ctx.enter_context(nc.semaphore(name))

        weights = build_constants(nc, sb, sem, w_self, b_self, w_neigh, b_neigh)
        with ExitStack() as fast:
            build_common_case(nc, fast, weights, x, src, dst, out)
        with ExitStack() as general:
            build_general_case(nc, general, weights, x, src, dst, out)


class Constants:
    pass


def build_constants(nc, sb, sem, w_self, b_self, w_neigh, b_neigh):
    k = Constants()
    k.column = sb("column", [P, P])
    k.partition = sb("partition", [P, 1])
    k.identity = sb("identity", [P, P])
    k.before = sb("before", [P, P])
    k.ones_bf = sb("ones_bf", [P, P], BF16)
    k.ones = sb("ones", [P, P])
    k.eps = sb("eps", [P, 1])
    k.ws = sb("ws", [P, DIM])
    k.wn = sb("wn", [P, DIM])
    k.wsum = sb("wsum", [P, DIM])
    k.ws_t = sb("ws_t", [P, DIM])
    k.wn_t = sb("wn_t", [P, DIM])
    k.wsum_t = sb("wsum_t", [P, DIM])
    k.bn = sb("bn", [P, DIM])
    k.bs_row = sb("bs_row", [1, DIM])
    k.bn_row = sb("bn_row", [1, DIM])
    k.bsn_row = sb("bsn_row", [1, DIM])
    k.bsn_rest = sb("bsn_rest", [1, 2, DIM])
    k.bsn_part = sb("bsn_part", [1, 3, DIM], BF16)
    k.bsn3 = sb("bsn3", [3, DIM], BF16)
    k.needs_general = sb("needs_general", [1, 1], INT32)
    return_sems(k, sem)
    k.inputs = (w_self, b_self, w_neigh, b_neigh)
    return k


def return_sems(k, sem):
    k.iotas = sem("iotas")
    k.weights_landed = sem("weights_landed")
    k.bn_landed = sem("bn_landed")
    k.consts_made = sem("consts_made")
    k.weights_turned = sem("weights_turned")
    k.weights_copied = sem("weights_copied")
    k.parts_made = sem("parts_made")
    k.parts_landed = sem("parts_landed")


def build_common_case(nc, ctx, k, x, src, dst, out):
    def sb(name, shape, dtype=FP32):
        return ctx.enter_context(nc.sbuf_tensor(name, shape, dtype))

    def sem(name):
        return ctx.enter_context(nc.semaphore(name))

    def scratch(name, shape, dtype):
        return nc.dram_tensor(name, shape, dtype, kind="Internal").ap()

    w_self, b_self, w_neigh, b_neigh = k.inputs

    src_padded = scratch("src_padded", (EDGES + PAD, 1), INT32)
    dst_padded = scratch("dst_padded", (EDGES + PAD, 1), INT32)
    kept_upto_dram = scratch("kept_upto_dram", (BLOCKS, BLOCK), FP32)
    ends_dram = scratch("ends_dram", (1, EDGE_ROWS * 2 * BLOCKS_PER_ROW), FP32)
    table_dram = scratch("table_dram", (ENTRIES, TABLE), INT32)
    bounds_dram = scratch("bounds_dram", (ENTRIES, 2), FP32)

    edge_src = sb("edge_src", [EDGE_ROWS, EDGE_COLS], INT32)
    edge_dst = sb("edge_dst", [EDGE_ROWS, EDGE_COLS + 1], INT32)
    flag_a = sb("flag_a", [EDGE_ROWS, EDGE_COLS])
    flag_b = sb("flag_b", [EDGE_ROWS, EDGE_COLS])
    zeros = sb("zeros", [EDGE_ROWS, EDGE_COLS])
    kept_upto = sb("kept_upto", [EDGE_ROWS, EDGE_COLS])
    pad_src = sb("pad_src", [1, PAD], INT32)
    pad_dst = sb("pad_dst", [1, PAD], INT32)
    rows_before = sb("rows_before", [EDGE_ROWS, 1])
    ends = sb("ends", [EDGE_ROWS, 2, BLOCKS_PER_ROW])
    all_ends = sb("all_ends", [SPREAD, EDGE_ROWS, 2, BLOCKS_PER_ROW])
    below = sb("below", [SPREAD, EDGE_ROWS * BLOCKS_PER_ROW])
    limit = sb("limit", [SPREAD, COLUMNS])
    entry = sb("entry", [SPREAD, COLUMNS])
    counts = sb("counts", [SPREAD, 2, COLUMNS])
    block = sb("block", [SPREAD, 2, COLUMNS])
    block_index = sb("block_index", [SPREAD, 2, COLUMNS], INT32)
    in_block = sb("in_block", [SPREAD, 2, COLUMNS])
    kept_block = sb("kept_block", [SPREAD, COLUMNS, BLOCK])
    dst_block = sb("dst_block", [SPREAD, COLUMNS, BLOCK], INT32)
    place = sb("place", [SPREAD, 2, COLUMNS])
    place_index = sb("place_index", [SPREAD, 2, COLUMNS], INT32)
    packed_before = sb("packed_before", [SPREAD, COLUMNS])
    first_int = sb("first_int", [SPREAD, COLUMNS], INT32)
    drift = sb("drift", [SPREAD, COLUMNS])
    drift_in = sb("drift_in", [SPREAD, COLUMNS])
    first = sb("first", [SPREAD, COLUMNS])
    ring_slot = sb("ring_slot", [SPREAD, SPAN, COLUMNS])
    table = sb("table", [SPREAD, COLUMNS, TABLE], INT32)
    table_row = sb("table_row", [1, ENTRIES, TABLE], INT32)
    bounds = sb("bounds", [SPREAD, COLUMNS, 2])
    bounds_row = sb("bounds_row", [1, ENTRIES, 2])
    cover = sb("cover", [1, ENTRIES])
    checks = sb("checks", [P, 6])
    check_sums = sb("check_sums", [1, 6])
    check_all = sb("check_all", [1, 2])
    window_checks = sb("window_checks", [SPREAD, COLUMNS])

    win_src = sb("win_src", [SPREAD, COLUMNS, WINDOW], INT32)
    win_dst = sb("win_dst", [SPREAD, COLUMNS, WINDOW + 1], INT32)
    win_loop = sb("win_loop", [SPREAD, COLUMNS, WINDOW])
    win_last = sb("win_last", [SPREAD, COLUMNS, WINDOW])
    win_gone = sb("win_gone", [SPREAD, COLUMNS, WINDOW])
    pair = [sb(f"pair{i}", [SPREAD, COLUMNS, WINDOW], INT32) for i in range(2)]
    shift = [sb(f"shift{i}", [SPREAD, COLUMNS, WINDOW], INT32) for i in range(2)]
    moves = sb("moves", [SPREAD, COLUMNS, WINDOW], INT32)
    pair_field = sb("pair_field", [SPREAD, 2, COLUMNS, P], INT32)
    pair_value = sb("pair_value", [SPREAD, 2, COLUMNS, P])
    chunk_src = sb("chunk_src", [P, ENTRIES], INT32)
    chunk_dst = sb("chunk_dst", [P, ENTRIES + 1])

    column3 = sb("column3", [P, SPAN, P])
    tile_base = sb("tile_base", [P, TILES])
    staged = sb("staged", [P, RING], INT32)
    ring = sb("ring", [P, RING, ROW])
    x_in = [sb(f"x_in{i}", [P, TRIO, DIM]) for i in range(DEEP)]
    pick = [sb(f"pick{i}", [P, TRIO, SPAN, P]) for i in range(2)]
    sums = [sb(f"sums{i}", [P, TRIO, ROW]) for i in range(DEEP)]
    x_t = [sb(f"x_t{i}", [P, TRIO, P]) for i in range(2)]
    sums_t = [sb(f"sums_t{i}", [P, TRIO, P]) for i in range(2)]
    with_degree = [sb(f"with_degree{i}", [P, TRIO, DIM]) for i in range(2)]
    y = [sb(f"y{i}", [P, TRIO, DIM]) for i in range(2)]
    stats = [sb(f"stats{i}", [P, TRIO, 6]) for i in range(2)]
    mean_var = [sb(f"mean_var{i}", [P, TRIO, 2]) for i in range(2)]
    std = [sb(f"std{i}", [P, TRIO]) for i in range(2)]
    rstd = [sb(f"rstd{i}", [P, TRIO]) for i in range(2)]
    minus_mean = [sb(f"minus_mean{i}", [P, TRIO]) for i in range(2)]
    result = [sb(f"result{i}", [P, TRIO, DIM]) for i in range(DEEP)]

    bank = [ctx.enter_context(nc.psum_tensor(f"bank{i}", [P, 512], FP32)) for i in range(8)]
    sum_bank, xt_bank, st_bank, h_bank = bank[0:2], bank[2:4], bank[4:6], bank[6:8]

    edges_landed = sem("edges_landed")
    next_landed = sem("next_landed")
    next_set = sem("next_set")
    pads_set = sem("pads_set")
    padded_stored = sem("padded_stored")
    row_counts = sem("row_counts")
    rows_summed = sem("rows_summed")
    upto_done = sem("upto_done")
    upto_stored = sem("upto_stored")
    ends_done = sem("ends_done")
    ends_stored = sem("ends_stored")
    ends_landed = sem("ends_landed")
    blocks_found = sem("blocks_found")
    block_landed = [sem(f"block_landed{i}") for i in range(2 * COLUMNS)]
    places_found = sem("places_found")
    window_landed = [sem(f"window_landed{i}") for i in range(2 * COLUMNS)]
    table_done = sem("table_done")
    table_stored = sem("table_stored")
    table_landed = sem("table_landed")
    fields_done = sem("fields_done")
    fields_turned = sem("fields_turned")
    chunks_known = sem("chunks_known")
    dve_order = sem("dve_order")
    checks_done = sem("checks_done")
    checks_summed = sem("checks_summed")
    gathered = [sem(f"gathered{i}") for i in range(GATHER_SEMS)]
    stage_done = sem("stage_done")
    slots_free = sem("slots_free")
    ones_set = sem("ones_set")
    x_landed = [sem(f"x_landed{i}") for i in range(DEEP)]
    pick_built = sem("pick_built")
    tiles_summed = sem("tiles_summed")
    sums_copied = sem("sums_copied")
    st_turned = sem("st_turned")
    st_copied = sem("st_copied")
    xt_turned = sem("xt_turned")
    xt_copied = sem("xt_copied")
    h_done = sem("h_done")
    h_used = sem("h_used")
    y_done = sem("y_done")
    stats_done = sem("stats_done")
    mean_var_done = sem("mean_var_done")
    std_done = sem("std_done")
    rstd_done = sem("rstd_done")
    norm_ready = sem("norm_ready")
    result_done = sem("result_done")
    stored = [sem(f"stored{i}") for i in range(DEEP)]

    def tiles_of(tau):
        return (1, LAST_ROWS) if isinstance(tau, int) and tau == TRIOS - 1 else (TRIO, P)

    def rows_of(dram, tau):
        tiles, rows = tiles_of(tau)
        if tiles == 1:
            return dram[NODES - rows:NODES, :].rearrange("(t p) d -> p t d", t=1)
        return dram[bass.ds(tau * (TRIO * P), TRIO * P), :].rearrange("(t p) d -> p t d", t=TRIO)


    def load_table(engine, tau, tiles):
        registers = [engine.alloc_register(nc.get_next_instruction_name().replace("I-", "word")) for _ in range(tiles * TABLE)]
        engine.load(registers, table_row[:].rearrange("a e w -> a (e w)")[:, bass.ds(tau * (TRIO * TABLE), tiles * TABLE)])
        return [registers[q * TABLE:(q + 1) * TABLE] for q in range(tiles)]

    def free_table(engine, table_registers):
        for register in sum(table_registers, []):
            engine.free_register(register)

    with nc.Block() as block_:
        @block_.sync
        def _(sp):
            sp.dma_start(edge_src[:], src.rearrange("(p e) -> p e", p=EDGE_ROWS)).then_inc(edges_landed, 16)
            sp.dma_start(edge_dst[:, 0:EDGE_COLS], dst.rearrange("(p e) -> p e", p=EDGE_ROWS)).then_inc(edges_landed, 16)
            sp.wait_ge(next_set, 1)
            sp.dma_start(edge_dst[0:EDGE_ROWS - 1, EDGE_COLS:EDGE_COLS + 1],
                         dst.rearrange("(p e) -> p e", p=EDGE_ROWS)[1:EDGE_ROWS, 0:1],
                         allow_slow_non_contiguous=True).then_inc(next_landed, 16)
            sp.dma_start(k.ws[:], w_self).then_inc(k.weights_landed, 16)
            sp.dma_start(k.wn[:], w_neigh).then_inc(k.weights_landed, 16)
            sp.dma_start(k.bs_row[:], b_self.rearrange("(a d) -> a d", a=1)).then_inc(k.weights_landed, 16)
            sp.dma_start(k.bn_row[:], b_neigh.rearrange("(a d) -> a d", a=1)).then_inc(k.weights_landed, 16)
            sp.dma_start(k.bn[:], b_neigh.rearrange("(a d) -> a d", a=1).partition_broadcast(P)).then_inc(k.bn_landed, 16)
            sp.wait_ge(edges_landed, 32)
            sp.dma_start(src_padded[0:EDGES, :].rearrange("(p e) o -> p (e o)", p=EDGE_ROWS), edge_src[:]).then_inc(padded_stored, 16)
            sp.dma_start(dst_padded[0:EDGES, :].rearrange("(p e) o -> p (e o)", p=EDGE_ROWS),
                         edge_dst[:, 0:EDGE_COLS]).then_inc(padded_stored, 16)
            sp.wait_ge(pads_set, 2)
            sp.dma_start(src_padded[EDGES:EDGES + PAD, :].rearrange("e o -> o e"), pad_src[:]).then_inc(padded_stored, 16)
            sp.dma_start(dst_padded[EDGES:EDGES + PAD, :].rearrange("e o -> o e"), pad_dst[:]).then_inc(padded_stored, 16)
            for tau in range(DEEP):
                sp.dma_start(x_in[tau][:], rows_of(x, tau)).then_inc(x_landed[tau], 16)
            sp.wait_ge(ends_done, 1)
            sp.dma_start(ends_dram[0, :].rearrange("(p w) -> p w", p=EDGE_ROWS), ends[:].rearrange("p a b -> p (a b)")).then_inc(ends_stored, 16)
            sp.wait_ge(upto_done, 1)
            sp.dma_start(kept_upto_dram.rearrange("(p b) e -> p (b e)", p=EDGE_ROWS), kept_upto[:]).then_inc(upto_stored, 16)
            sp.wait_ge(ends_stored, 16)
            sp.dma_start(all_ends[:].rearrange("p a b c -> p (a b c)"), ends_dram.partition_broadcast(SPREAD)).then_inc(ends_landed, 16)
            sp.wait_ge(k.parts_made, 3)
            sp.dma_start(k.bsn3[:], k.bsn_part[:]).then_inc(k.parts_landed, 16)
            sp.wait_ge(table_done, 1)
            for mine, dram in ((table, table_dram), (bounds, bounds_dram)):
                sp.dma_start(dram.rearrange("(j p) w -> p j w", p=SPREAD), mine[:]).then_inc(table_stored, 16)
            sp.wait_ge(table_stored, 32)
            for mine, dram in ((table_row, table_dram), (bounds_row, bounds_dram)):
                sp.dma_start(mine[:].rearrange("a e w -> a (e w)"),
                             dram.rearrange("e w -> (e w)").rearrange("(a w) -> a w", a=1)).then_inc(table_landed, 16)

            def load_x(t, u):
                tau = t + u
                sp.wait_ge(y_done, tau - DEEP + 1)
                sp.dma_start(x_in[u % DEEP][0:tiles_of(tau)[1], 0:tiles_of(tau)[0], :], rows_of(x, tau)).then_inc(x_landed[u % DEEP], 16)

            with sp.Fori(DEEP, LOOPED - DEEP + 1, DEEP) as t:
                for u in range(DEEP):
                    load_x(t, u)
            for u in range(TRIOS - LOOPED):
                load_x(LOOPED, u)

        @block_.gpsimd
        def _(pool):
            def iota(out_, pattern, multiplier):
                return nc.gpsimd.iota(out_, pattern, base=0, channel_multiplier=multiplier, allow_small_or_imprecise_dtypes=True)

            iota(k.column[:], [[1, P]], 0).then_inc(k.iotas, 1)
            iota(k.partition[:], [[1, 1]], 1).then_inc(k.iotas, 1)
            iota(limit[:], [[P * SPREAD, COLUMNS]], P).then_inc(k.iotas, 1)
            iota(entry[:], [[SPREAD, COLUMNS]], 1).then_inc(k.iotas, 1)
            iota(column3[:], [[0, SPAN], [1, P]], 0).then_inc(k.iotas, 1)
            iota(tile_base[:], [[P, TILES]], 0).then_inc(k.iotas, 1)
            nc.gpsimd.memset(ring[:, :, DIM:DIM + 1], 1.0).then_inc(ones_set, 1)
            pool.wait_ge(upto_stored, 16)
            for a in range(2):
                for j in range(COLUMNS):
                    pool.wait_ge(blocks_found, a + 1)
                    if a == 0:
                        nc.gpsimd.indirect_dma_start(kept_block[:, j, :], None, kept_upto_dram,
                                                     bass.IndirectOffsetOnAxis(ap=block_index[:, a, j:j + 1], axis=0)
                                                     ).then_inc(block_landed[j], 16)
                    else:
                        nc.gpsimd.indirect_dma_start(dst_block[:, j, :], None, dst.rearrange("(b e) -> b e", e=BLOCK),
                                                     bass.IndirectOffsetOnAxis(ap=block_index[:, a, j:j + 1], axis=0)
                                                     ).then_inc(block_landed[COLUMNS + j], 16)
            pool.wait_ge(padded_stored, 64)
            pool.wait_ge(places_found, 1)
            for j in range(COLUMNS):
                nc.gpsimd.indirect_dma_start(win_src[:, j, :], None, src_padded,
                                             bass.IndirectOffsetOnAxis(ap=place_index[:, 0, j:j + 1], axis=0)
                                             ).then_inc(window_landed[2 * j], 16)
                nc.gpsimd.indirect_dma_start(win_dst[:, j, :], None, dst_padded,
                                             bass.IndirectOffsetOnAxis(ap=place_index[:, 0, j:j + 1], axis=0)
                                             ).then_inc(window_landed[2 * j + 1], 16)

            def gather(r, slot):
                round_ = slot // GATHER_SEMS
                if not (isinstance(r, int) and r == 0 and round_ == 0):
                    pool.wait_ge(gathered[slot % GATHER_SEMS], r * (16 * (RING // GATHER_SEMS)) + 16 * round_)
                    pool.sem_inc(slots_free, 1)
                nc.gpsimd.indirect_dma_start(ring[:, slot, 0:DIM], None, x,
                                             bass.IndirectOffsetOnAxis(ap=staged[:, slot:slot + 1], axis=0)
                                             ).then_inc(gathered[slot % GATHER_SEMS], 16)

            def stage(r, h, count):
                if not (isinstance(r, int) and r == 0):
                    pool.wait_ge(tiles_summed, r * RING + (h * STAGE + STAGE - 1 - RING + DRIFT + 1))
                nc.gpsimd.tensor_copy(staged[:, h * STAGE:h * STAGE + count],
                                      chunk_src[:, bass.ds(r * RING + h * STAGE, count)]).then_inc(stage_done, 1)
                pool.wait_ge(stage_done, r * (RING // STAGE) + h + 1)
                for slot in range(h * STAGE, h * STAGE + count):
                    gather(r, slot)

            pool.wait_ge(chunks_known, 2)
            for h in range(RING // STAGE):
                stage(0, h, STAGE)
            pool.wait_ge(chunks_known, 4)
            with pool.Fori(1, CHUNKS // RING, 1) as r:
                for h in range(RING // STAGE):
                    stage(r, h, STAGE)
            stage(CHUNKS // RING, 0, CHUNKS % RING)

        @block_.vector
        def _(dve):
            chain = [0]

            def link(ins):
                chain[0] += 1
                ins.then_inc(dve_order, 1)
                dve.wait_ge(dve_order, chain[0])

            v = nc.vector
            v.memset(edge_dst[:, EDGE_COLS:EDGE_COLS + 1], NO_NODE).then_inc(next_set, 1)
            v.memset(pad_src[:], 0).then_inc(pads_set, 1)
            v.memset(pad_dst[:], NO_NODE).then_inc(pads_set, 1)
            v.memset(k.ones[:], 1.0)
            v.memset(k.eps[:], EPS)
            v.memset(zeros[:], 0.0)
            v.memset(checks[:], 0.0)
            v.memset(chunk_dst[:, ENTRIES:ENTRIES + 1], float(NO_NODE))
            link(v.memset(k.ones_bf[:], 1.0))
            dve.wait_ge(k.iotas, 2)
            v.tensor_scalar(k.before[:], k.column[:], k.partition[:, 0:1], None, ALU.is_gt)
            v.tensor_scalar(k.identity[:], k.column[:], k.partition[:, 0:1], None, ALU.is_equal).then_inc(k.consts_made, 1)

            dve.wait_ge(edges_landed, 32)
            v.tensor_tensor(flag_a[:], edge_src[:], edge_dst[:, 0:EDGE_COLS], ALU.is_equal)
            dve.wait_ge(next_landed, 16)
            link(v.tensor_tensor(flag_b[:], edge_dst[:, 1:EDGE_COLS + 1], edge_dst[:, 0:EDGE_COLS], ALU.not_equal))
            link(v.tensor_tensor(flag_a[:], flag_a[:], flag_b[:], ALU.mult))
            link(v.tensor_scalar(flag_b[:], flag_a[:], -1.0, 1.0, ALU.mult, ALU.add))
            v.tensor_tensor_scan(kept_upto[:], flag_b[:], zeros[:], 0.0, ALU.add, ALU.add).then_inc(row_counts, 1)
            dve.wait_ge(rows_summed, 1)
            link(v.tensor_copy(rows_before[:], bank[0][0:EDGE_ROWS, 0:1]))
            link(v.tensor_copy(checks[0:EDGE_ROWS, 4:5], kept_upto[:, EDGE_COLS - 1:EDGE_COLS]))
            v.tensor_scalar(kept_upto[:], kept_upto[:], rows_before[:, 0:1], None, ALU.add).then_inc(upto_done, 1)
            dve.wait_ge(upto_done, 1)
            v.tensor_copy(ends[:, 0, :], kept_upto[:, BLOCK - 1:EDGE_COLS:BLOCK])
            v.tensor_copy(ends[:, 1, :], edge_dst[:, BLOCK - 1:EDGE_COLS:BLOCK]).then_inc(ends_done, 1)
            dve.wait_ge(k.weights_landed, 64)
            v.tensor_tensor(k.wsum[:], k.ws[:], k.wn[:], ALU.add).then_inc(k.consts_made, 1)
            link(v.tensor_tensor(k.bsn_row[:], k.bs_row[:], k.bn_row[:], ALU.add))
            v.tensor_copy(k.bsn_part[:, 0, :], k.bsn_row[:]).then_inc(k.parts_made, 1)
            dve.wait_ge(k.parts_made, 1)
            link(v.tensor_tensor(k.bsn_rest[:, 0, :], k.bsn_row[:], k.bsn_part[:, 0, :], ALU.subtract))
            v.tensor_copy(k.bsn_part[:, 1, :], k.bsn_rest[:, 0, :]).then_inc(k.parts_made, 1)
            dve.wait_ge(k.parts_made, 2)
            link(v.tensor_tensor(k.bsn_rest[:, 1, :], k.bsn_rest[:, 0, :], k.bsn_part[:, 1, :], ALU.subtract))
            v.tensor_copy(k.bsn_part[:, 2, :], k.bsn_rest[:, 1, :]).then_inc(k.parts_made, 1)

            dve.wait_ge(ends_landed, 16)
            dve.wait_ge(k.iotas, 6)
            for a, less in ((0, ALU.is_le), (1, ALU.is_lt)):
                for j in range(COLUMNS):
                    link(v.tensor_scalar(below[:].rearrange("p (a b) -> p a b", a=EDGE_ROWS), all_ends[:, :, a, :],
                                         limit[:, j:j + 1], 0.0, less, ALU.add, accum_out=counts[:, a, j:j + 1]))
                link(v.tensor_scalar(block[:, a, :], counts[:, a, :], float(BLOCKS - 1), None, ALU.min))
                v.tensor_copy(block_index[:, a, :], block[:, a, :]).then_inc(blocks_found, 1)
            def find_places(a):
                blocks_, less = ((kept_block, ALU.is_le), (dst_block, ALU.is_lt))[a]
                for j in range(COLUMNS):
                    dve.wait_ge(block_landed[a * COLUMNS + j], 16)
                    link(v.tensor_scalar(below[:, 0:BLOCK], blocks_[:, j, :], limit[:, j:j + 1], 0.0, less, ALU.add,
                                         accum_out=in_block[:, a, j:j + 1]))
                link(v.scalar_tensor_tensor(place[:, a, :], block[:, a, :], float(BLOCK), in_block[:, a, :], ALU.mult, ALU.add))
                v.tensor_copy(place_index[:, a, :], place[:, a, :]).then_inc(places_found, 1)

            find_places(0)
            find_places(1)

            link(v.tensor_tensor(packed_before[:], place[:, 1, :], limit[:], ALU.subtract))
            dve.wait_ge(places_found, 2)
            link(v.tensor_scalar(first_int[:], place_index[:, 1, :], 7, None, ALU.logical_shift_right))
            link(v.tensor_copy(first[:], first_int[:]))
            link(v.tensor_tensor(first[:], first[:], entry[:], ALU.subtract))
            link(v.tensor_tensor(drift[:], first[:], entry[:], ALU.subtract))
            link(v.tensor_scalar(drift_in[:], drift[:], float(-DRIFT), float(DRIFT), ALU.max, ALU.min))
            link(v.tensor_tensor(first[:], drift_in[:], entry[:], ALU.add))
            link(v.tensor_scalar(first[:], first[:], 0.0, float(CHUNKS - 1), ALU.max, ALU.min))
            for s in range(SPAN):
                link(v.tensor_scalar(ring_slot[:, s, :], first[:], float(s), None, ALU.add))
            for lap in range((CHUNKS + SPAN) // RING, 0, -1):
                link(v.tensor_scalar(below[:, 0:SPAN * COLUMNS], ring_slot[:].rearrange("p s j -> p (s j)"), float(lap * RING),
                                     float(-RING * lap), ALU.is_ge, ALU.mult))
                link(v.tensor_tensor(ring_slot[:].rearrange("p s j -> p (s j)"), ring_slot[:].rearrange("p s j -> p (s j)"),
                                     below[:, 0:SPAN * COLUMNS], ALU.add))
            for s in range(SPAN):
                v.tensor_scalar(table[:, :, s], ring_slot[:, s, :], float(ROW), None, ALU.mult)
            v.tensor_copy(table[:, :, SPAN], first[:])
            v.tensor_copy(bounds[:, :, 0], packed_before[:])
            v.tensor_scalar(bounds[:, :, 1], first[:], float(P), float(SPAN * P), ALU.mult, ALU.add).then_inc(table_done, 1)

            def pack(j0, j1):
                js = slice(j0, j1)
                for j in range(j0, j1):
                    dve.wait_ge(window_landed[2 * j], 16)
                    dve.wait_ge(window_landed[2 * j + 1], 16)
                v.tensor_tensor(win_loop[:, js, :], win_src[:, js, :], win_dst[:, js, 0:WINDOW], ALU.is_equal)
                v.tensor_tensor(win_last[:, js, :], win_dst[:, js, 1:WINDOW + 1], win_dst[:, js, 0:WINDOW], ALU.not_equal)
                link(v.scalar_tensor_tensor(pair[0][:, js, :], win_src[:, js, :], 16, win_dst[:, js, 0:WINDOW],
                                            ALU.logical_shift_left, ALU.bitwise_or))
                link(v.tensor_tensor(win_loop[:, js, :], win_loop[:, js, :], win_last[:, js, :], ALU.mult))
                for j in range(j0, j1):
                    ins = v.tensor_tensor_scan(win_gone[:, j, :], win_loop[:, j, :], zeros[0:SPREAD, 0:WINDOW], 0.0, ALU.add, ALU.add)
                link(ins)
                v.tensor_scalar(checks_view(j0, j1), win_gone[:, js, WINDOW - 1], float(WINDOW - P), None, ALU.is_gt)
                link(v.tensor_scalar(win_last[:, js, :], win_loop[:, js, :], -1.0, 1.0, ALU.mult, ALU.add))
                link(v.tensor_tensor(shift[0][:, js, :], win_gone[:, js, :], win_last[:, js, :], ALU.mult))
                for bit in range(SHIFT_BITS):
                    step = 1 << bit
                    old, new = bit % 2, 1 - bit % 2
                    v.tensor_copy(pair[new][:, js, :], pair[old][:, js, :])
                    link(v.tensor_scalar(moves[:, js, :], shift[old][:, js, :], step, None, ALU.bitwise_and))
                    link(v.scalar_tensor_tensor(shift[new][:, js, :], moves[:, js, :], 0.0, shift[old][:, js, :], ALU.is_equal, ALU.mult))
                    v.copy_predicated(pair[new][:, js, 0:WINDOW - step], moves[:, js, step:WINDOW], pair[old][:, js, step:WINDOW])
                    link(v.copy_predicated(shift[new][:, js, 0:WINDOW - step], moves[:, js, step:WINDOW], shift[old][:, js, step:WINDOW]))
                final = pair[SHIFT_BITS % 2]
                v.tensor_scalar(pair_field[:, 0, js, :], final[:, js, 0:P], 16, None, ALU.logical_shift_right)
                link(v.tensor_scalar(pair_field[:, 1, js, :], final[:, js, 0:P], 0xFFFF, None, ALU.bitwise_and))
                v.tensor_copy(pair_value[:, :, js, :], pair_field[:, :, js, :]).then_inc(fields_done, 1)

            def checks_view(j0, j1):
                return window_checks[:, j0:j1]

            pack(0, 1)
            dve.wait_ge(fields_turned, 1)
            v.tensor_copy(chunk_src[:, 0:SPREAD], bank[0][:, 0:SPREAD]).then_inc(chunks_known, 1)
            v.tensor_copy(chunk_dst[:, 0:SPREAD], bank[0][:, SPREAD:2 * SPREAD]).then_inc(chunks_known, 1)
            pack(1, COLUMNS)
            dve.wait_ge(fields_turned, 2)
            v.tensor_copy(chunk_src[:, SPREAD:ENTRIES], bank[0][:, 0:ENTRIES - SPREAD]).then_inc(chunks_known, 1)
            v.tensor_copy(chunk_dst[:, SPREAD:ENTRIES], bank[1][:, 0:ENTRIES - SPREAD]).then_inc(chunks_known, 1)
            dve.wait_ge(chunks_known, 4)

            link(v.tensor_tensor(flag_a[:], edge_dst[:, 1:EDGE_COLS + 1], edge_dst[:, 0:EDGE_COLS], ALU.is_lt))
            v.reduce_sum(checks[0:EDGE_ROWS, 0:1], flag_a[:], AXIS_X)
            v.reduce_sum(checks[0:SPREAD, 1:2], window_checks[:], AXIS_X)
            link(v.tensor_tensor(below[:, 0:COLUMNS], drift[:], drift_in[:], ALU.not_equal))
            link(v.reduce_sum(checks[0:SPREAD, 2:3], below[:, 0:COLUMNS], AXIS_X))
            dve.wait_ge(table_landed, 32)
            link(v.tensor_tensor(cover[:, 0:TILES], bounds_row[:, 1:TILES + 1, 0], bounds_row[:, 0:TILES, 1], ALU.is_gt))
            link(v.reduce_sum(check_all[:, 1:2], cover[:, 0:TILES], AXIS_X))
            v.tensor_copy(checks[0:1, 3:4], check_all[:, 1:2]).then_inc(checks_done, 1)
            dve.wait_ge(checks_summed, 1)
            link(v.tensor_copy(check_sums[:], bank[0][0:1, 0:6]))
            link(v.tensor_scalar(check_sums[:, 4:5], check_sums[:, 4:5], float(PACKED), None, ALU.not_equal))
            link(v.reduce_sum(check_all[:, 0:1], check_sums[:], AXIS_X))
            link(v.tensor_scalar(k.needs_general[:], check_all[:, 0:1], 0.0, None, ALU.is_gt))

            def build_pick(t, u):
                tau = t + u
                if not (isinstance(tau, int) and tau < 2):
                    dve.wait_ge(tiles_summed, (tau - 1) * TRIO)
                tiles, _ = tiles_of(tau)
                words = load_table(dve, tau, tiles)
                for q in range(tiles):
                    n = tau * TRIO + q
                    first_chunk = dve.snap(words[q][SPAN], donate=True, min_val=0, max_val=CHUNKS - 1)
                    ins = v.scalar_tensor_tensor(pick[u % 2][:, q, :, :], column3[:], tile_base[:, bass.ds(n, 1)],
                                                 chunk_dst[:, bass.ds(first_chunk, SPAN)].unsqueeze(2).to_broadcast([P, SPAN, P]),
                                                 ALU.add, ALU.is_equal)
                free_table(dve, words)
                ins.then_inc(pick_built, 1)

            def residual(t, u):
                tau, b = t + u, u % 2
                tiles, rows = tiles_of(tau)
                dve.wait_ge(h_done, tau + 1)
                h = h_bank[b][:, 0:TRIO * DIM].rearrange("p (q d) -> p q d", q=TRIO)
                for q in range(tiles):
                    ins = v.scalar_tensor_tensor(with_degree[b][0:rows, q, :], k.bn[0:rows, :], sums[u % DEEP][0:rows, q, DIM:DIM + 1],
                                                 h[0:rows, q, :], ALU.mult, ALU.add)
                ins.then_inc(h_used, 1)
                dve.wait_ge(h_used, tau + 1)
                if not (isinstance(tau, int) and tau < 2):
                    dve.wait_ge(result_done, tau - 1)
                v.scalar_tensor_tensor(y[b][0:rows, 0:tiles, :], with_degree[b][0:rows, 0:tiles, :], 0.0,
                                       x_in[u % DEEP][0:rows, 0:tiles, :], ALU.max, ALU.add).then_inc(y_done, 1)
                dve.wait_ge(y_done, tau + 1)
                for q in range(tiles):
                    ins = v.bn_stats(stats[b][0:rows, q, :], y[b][0:rows, q, :])
                ins.then_inc(stats_done, 1)

            def aggregate(t, u):
                tau, b = t + u, u % 2
                tiles, rows = tiles_of(tau)
                for q in range(tiles):
                    ins = v.bn_aggr(mean_var[b][0:rows, q, :], stats[b][0:rows, q, :])
                ins.then_inc(mean_var_done, 1)

            def scales(t, u):
                tau, b = t + u, u % 2
                tiles, rows = tiles_of(tau)
                if not (isinstance(tau, int) and tau + 1 >= TRIOS):
                    dve.wait_ge(stats_done, tau + 2)
                dve.wait_ge(std_done, tau + 1)
                v.reciprocal(rstd[b][0:rows, 0:tiles], std[b][0:rows, 0:tiles]).then_inc(rstd_done, 1)
                dve.wait_ge(rstd_done, tau + 1)
                v.scalar_tensor_tensor(minus_mean[b][0:rows, 0:tiles], mean_var[b][0:rows, 0:tiles, 0], -1.0,
                                       rstd[b][0:rows, 0:tiles], ALU.mult, ALU.mult).then_inc(norm_ready, 1)

            def step(t, u):
                tau = t + u
                known = isinstance(tau, int)
                if not known or tau + 2 < TRIOS:
                    build_pick(t, u + 2)
                if not known or 1 <= tau <= TRIOS:
                    residual(t, u - 1)
                if known and tau == 1:
                    dve.wait_ge(stats_done, 1)
                if not known or tau >= 2:
                    scales(t, u - 2)
                if not known or 1 <= tau <= TRIOS:
                    aggregate(t, u - 1)

            dve.wait_ge(k.bn_landed, 16)
            build_pick(0, 0)
            build_pick(0, 1)
            for u in range(DEEP):
                step(0, u)
            with dve.Fori(DEEP, LOOPED - DEEP + 1, DEEP) as t:
                for u in range(DEEP):
                    step(t, u)
            for u in range(TRIOS + 2 - LOOPED):
                step(LOOPED, u)

        @block_.tensor
        def _(pe):
            mm = nc.tensor.matmul
            pe.wait_ge(k.consts_made, 1)
            pe.wait_ge(row_counts, 1)
            mm(bank[0][0:EDGE_ROWS, 0:1], k.before[0:EDGE_ROWS, 0:EDGE_ROWS], kept_upto[:, EDGE_COLS - 1:EDGE_COLS],
               start=True, stop=True).then_inc(rows_summed, 1)
            pe.wait_ge(k.consts_made, 2)
            for i, w in enumerate((k.ws, k.wn, k.wsum)):
                nc.tensor.transpose(bank[2 + i][:, 0:P], w[:], k.identity[:]).then_inc(k.weights_turned, 1)
            pe.wait_ge(fields_done, 1)
            nc.tensor.transpose(bank[0][:, 0:SPREAD], pair_value[:, 0, 0, :], k.identity[0:SPREAD, 0:SPREAD])
            nc.tensor.transpose(bank[0][:, SPREAD:2 * SPREAD], pair_value[:, 1, 0, :],
                                k.identity[0:SPREAD, 0:SPREAD]).then_inc(fields_turned, 1)
            pe.wait_ge(fields_done, 2)
            for a in range(2):
                for j in range(1, COLUMNS):
                    ins = nc.tensor.transpose(bank[a][:, (j - 1) * SPREAD:j * SPREAD], pair_value[:, a, j, :],
                                              k.identity[0:SPREAD, 0:SPREAD])
            ins.then_inc(fields_turned, 1)
            pe.wait_ge(checks_done, 1)
            mm(bank[0][0:1, 0:6], k.ones[:, 0:1], checks[:], start=True, stop=True).then_inc(checks_summed, 1)

            def turn_x(t, u):
                tau, b = t + u, u % 2
                tiles, rows = tiles_of(tau)
                pe.wait_ge(x_landed[u % DEEP], 4 * (t + u // DEEP * DEEP) + 16)
                if not (isinstance(tau, int) and tau < 2):
                    pe.wait_ge(xt_copied, tau - 1)
                for q in range(tiles):
                    ins = nc.tensor.transpose(xt_bank[b][:, q * P:q * P + rows], x_in[u % DEEP][0:rows, q, :], k.identity[0:rows, 0:rows])
                ins.then_inc(xt_turned, 1)

            def sum_rows(t, u):
                tau, b = t + u, u % 2
                known = isinstance(tau, int)
                pe.wait_ge(pick_built, tau + 1)
                if not known or tau >= 2:
                    pe.wait_ge(sums_copied, tau - 1)
                tiles, _ = tiles_of(tau)
                words = load_table(pe, tau, tiles)
                for q in range(tiles):
                    ahead = u * TRIO + q + DRIFT + SPAN - 1
                    n = tau * TRIO + q
                    if known and tau == 0 and q == 0:
                        for c in range(ahead):
                            pe.wait_ge(gathered[c % GATHER_SEMS], 16)
                    if not known or n + DRIFT + SPAN - 1 < CHUNKS:
                        pe.wait_ge(gathered[ahead % GATHER_SEMS], 4 * t + 16 * (ahead // GATHER_SEMS + 1))
                    slots = [pe.snap(words[q][s], donate=True, min_val=0, max_val=(RING - 1) * ROW) for s in range(SPAN)]
                    for s in range(SPAN):
                        ins = mm(sum_bank[b][:, q * ROW:q * ROW + DIM + 1], pick[b][:, q, s, :],
                                 ring[:].rearrange("p c w -> p (c w)")[:, bass.ds(slots[s], DIM + 1)],
                                 start=(s == 0), stop=(s == SPAN - 1))
                    ins.then_inc(tiles_summed, 1)
                free_table(pe, words)

            def turn_sums(t, u):
                tau, b = t + u, u % 2
                pe.wait_ge(sums_copied, tau + 1)
                if not (isinstance(tau, int) and tau < 2):
                    pe.wait_ge(st_copied, tau - 1)
                for q in range(tiles_of(tau)[0]):
                    ins = nc.tensor.transpose(st_bank[b][:, q * P:q * P + P], sums[u % DEEP][:, q, 0:DIM], k.identity[:])
                ins.then_inc(st_turned, 1)

            def products(t, u):
                tau, b = t + u, u % 2
                tiles, rows = tiles_of(tau)
                pe.wait_ge(st_copied, tau + 1)
                pe.wait_ge(xt_copied, tau + 1)
                if not (isinstance(tau, int) and tau < 2):
                    pe.wait_ge(h_used, tau - 1)
                for q in range(tiles):
                    h = h_bank[b][0:rows, q * DIM:q * DIM + DIM]
                    mm(h, k.ones_bf[0:3, 0:rows], k.bsn3[:], start=True, stop=False)
                    mm(h, x_t[b][:, q, 0:rows], k.wsum_t[:], start=False, stop=False)
                    ins = mm(h, sums_t[b][:, q, 0:rows], k.wn_t[:], start=False, stop=True)
                ins.then_inc(h_done, 1)

            def step(t, u):
                tau = t + u
                known = isinstance(tau, int)
                turn_sums(t, u)
                if not known or tau + 1 < TRIOS:
                    sum_rows(t, u + 1)
                    turn_x(t, u + 1)
                products(t, u)

            pe.wait_ge(k.weights_copied, 3)
            pe.wait_ge(k.parts_landed, 16)
            pe.wait_ge(table_landed, 32)
            pe.wait_ge(ones_set, 1)
            turn_x(0, 0)
            sum_rows(0, 0)
            for u in range(DEEP):
                step(0, u)
            with pe.Fori(DEEP, LOOPED - DEEP + 1, DEEP) as t:
                for u in range(DEEP):
                    step(t, u)
            for u in range(TRIOS - LOOPED):
                step(LOOPED, u)

        @block_.scalar
        def _(act):
            for i, w_t in enumerate((k.ws_t, k.wn_t, k.wsum_t)):
                act.wait_ge(k.weights_turned, i + 1)
                nc.scalar.copy(w_t[:], bank[2 + i][:, 0:P]).then_inc(k.weights_copied, 1)

            def copy_sums(t, u):
                tau, b = t + u, u % 2
                tiles, _ = tiles_of(tau)
                act.wait_ge(tiles_summed, tau * TRIO + tiles)
                nc.scalar.copy(sums[u % DEEP][:, 0:tiles, 0:DIM + 1],
                               sum_bank[b][:, 0:TRIO * ROW].rearrange("p (q w) -> p q w", q=TRIO)[:, 0:tiles, 0:DIM + 1]
                               ).then_inc(sums_copied, 1)

            def copy_sums_t(t, u):
                tau, b = t + u, u % 2
                tiles, _ = tiles_of(tau)
                act.wait_ge(st_turned, tau + 1)
                nc.scalar.copy(sums_t[b][:, 0:tiles, :], st_bank[b][:, 0:tiles * P].rearrange("p (q w) -> p q w", q=tiles)
                               ).then_inc(st_copied, 1)

            def copy_x_t(t, u):
                tau, b = t + u, u % 2
                tiles, rows = tiles_of(tau)
                act.wait_ge(xt_turned, tau + 1)
                nc.scalar.copy(x_t[b][:, 0:tiles, 0:rows],
                               xt_bank[b][:, 0:tiles * P].rearrange("p (q w) -> p q w", q=tiles)[:, :, 0:rows]
                               ).then_inc(xt_copied, 1)

            def deviation(t, u):
                tau, b = t + u, u % 2
                tiles, rows = tiles_of(tau)
                act.wait_ge(mean_var_done, tau + 1)
                nc.scalar.activation(std[b][0:rows, 0:tiles], mean_var[b][0:rows, 0:tiles, 1], ACT.Sqrt,
                                     bias=k.eps[0:rows, 0:1], scale=1.0).then_inc(std_done, 1)

            def normalise(t, u):
                tau, b = t + u, u % 2
                tiles, rows = tiles_of(tau)
                act.wait_ge(norm_ready, tau + 1)
                if not (isinstance(tau, int) and tau < DEEP):
                    act.wait_ge(stored[u % DEEP], 4 * (t + u // DEEP * DEEP))
                for q in range(tiles):
                    ins = nc.scalar.activation(result[u % DEEP][0:rows, q, :], y[b][0:rows, q, :], ACT.Identity,
                                               bias=minus_mean[b][0:rows, q:q + 1], scale=rstd[b][0:rows, q:q + 1])
                ins.then_inc(result_done, 1)
                act.wait_ge(result_done, tau + 1)
                act.dma_start(rows_of(out, tau), result[u % DEEP][0:rows, 0:tiles, :]).then_inc(stored[u % DEEP], 16)

            def step(t, u):
                tau = t + u
                known = isinstance(tau, int)
                if not known or tau >= 2:
                    deviation(t, u - 2)
                if not known or tau < TRIOS:
                    copy_sums_t(t, u)
                if not known or tau + 1 < TRIOS:
                    copy_sums(t, u + 1)
                    copy_x_t(t, u + 1)
                if not known or tau >= 2:
                    normalise(t, u - 2)

            copy_x_t(0, 0)
            copy_sums(0, 0)
            for u in range(DEEP):
                step(0, u)
            with act.Fori(DEEP, LOOPED - DEEP + 1, DEEP) as t:
                for u in range(DEEP):
                    step(t, u)
            for u in range(TRIOS + 2 - LOOPED):
                step(LOOPED, u)
            for i in range(DEEP):
                act.wait_ge(stored[i], 16 * len(range(i, TRIOS, DEEP)))


def build_general_case(nc, ctx, k, x, src, dst, out):
    def sb(name, shape, dtype=FP32):
        return ctx.enter_context(nc.sbuf_tensor(name, shape, dtype))

    def sem(name):
        return ctx.enter_context(nc.semaphore(name))

    sums_dram = nc.dram_tensor("sums_dram", (SUM_ROWS, ROW), FP32, kind="Internal").ap()
    zero_rows = sb("zero_rows", [P, ZERO_ROWS * ROW])
    bs = sb("bs", [P, DIM])
    dst_line = sb("dst_line", [GEN_EDGES, GEN_EDGES], INT32)
    dst_own = sb("dst_own", [GEN_EDGES, 1], INT32)
    src_own = sb("src_own", [GEN_EDGES, 1], INT32)
    dst_value = sb("dst_value", [GEN_EDGES, 1])
    spare_row = sb("spare_row", [GEN_EDGES, 1])
    earlier = sb("earlier", [GEN_EDGES, GEN_EDGES])
    same = sb("same", [GEN_EDGES, GEN_EDGES])
    same_earlier = sb("same_earlier", [GEN_EDGES, GEN_EDGES])
    repeats = sb("repeats", [GEN_EDGES, 1])
    is_repeat = sb("is_repeat", [GEN_EDGES, 1])
    to_spare = sb("to_spare", [GEN_EDGES, 1])
    moved = sb("moved", [GEN_EDGES, 1])
    target = sb("target", [GEN_EDGES, 1], INT32)
    rows = sb("rows", [GEN_EDGES, ROW])
    totals = sb("totals", [GEN_EDGES, ROW])
    x_rows = sb("x_rows", [GEN_ROWS, DIM])
    sum_rows = sb("sum_rows", [GEN_ROWS, ROW])
    x_turned = sb("x_turned", [P, 2, GEN_ROWS])
    biased = sb("biased", [GEN_ROWS, DIM])
    before_relu = sb("before_relu", [GEN_ROWS, DIM])
    y = sb("gen_y", [GEN_ROWS, DIM])
    stats = sb("gen_stats", [GEN_ROWS, 6])
    mean_var = sb("gen_mean_var", [GEN_ROWS, 2])
    std = sb("gen_std", [GEN_ROWS, 1])
    rstd = sb("gen_rstd", [GEN_ROWS, 1])
    result = sb("gen_result", [GEN_ROWS, DIM])
    totals_bank = ctx.enter_context(nc.psum_tensor("totals_bank", [P, 512], FP32))
    turn_bank = ctx.enter_context(nc.psum_tensor("turn_bank", [P, 512], FP32))
    h_bank = ctx.enter_context(nc.psum_tensor("gen_h_bank", [P, 512], FP32))

    zeros_set = sem("gen_zeros_set")
    zeroed = sem("gen_zeroed")
    bs_landed = sem("gen_bs_landed")
    step_landed = sem("gen_step_landed")
    rows_wanted = sem("gen_rows_wanted")
    rows_landed = sem("gen_rows_landed")
    same_done = sem("gen_same_done")
    target_done = sem("gen_target_done")
    totals_done = sem("gen_totals_done")
    totals_copied = sem("gen_totals_copied")
    adds_wanted = sem("gen_adds_wanted")
    added = sem("gen_added")
    order = sem("gen_order")
    tile_landed = sem("gen_tile_landed")
    turned = sem("gen_turned")
    turned_copied = sem("gen_turned_copied")
    h_done = sem("gen_h_done")
    var_done = sem("gen_var_done")
    std_done = sem("gen_std_done")
    result_done = sem("gen_result_done")
    stored = sem("gen_stored")

    EDGE_LINKS = 9
    TILE_LINKS = 5

    def only_if_needed(engine, program):
        needed = engine.value_load(k.needs_general[0:1, 0:1], min_val=0, max_val=1)
        with engine.If(needed > 0):
            program(engine)
            engine.nop()
        with engine.Else():
            engine.nop()
        engine.nop()

    with nc.Block() as block:
        @block.sync
        def _(sp):
            def program(sp):
                sp.dma_start(bs[:], k.inputs[1].rearrange("(a d) -> a d", a=1).partition_broadcast(P)).then_inc(bs_landed, 16)
                sp.wait_ge(zeros_set, 1)
                zero_view = sums_dram.rearrange("(z p r) w -> z p (r w)", p=P, r=ZERO_ROWS)
                for z in range(SUM_ROWS // (P * ZERO_ROWS)):
                    sp.dma_start(zero_view[z, :, :], zero_rows[:]).then_inc(zeroed, 16)
                sp.sem_inc(added, 16)
                with sp.Fori(0, GEN_STEPS, 1) as s:
                    edges = bass.ds(s * GEN_EDGES, GEN_EDGES)
                    sp.wait_ge(added, s * 16 + 16)
                    sp.dma_start(dst_line[:], dst[edges].rearrange("(a e) -> a e", a=1).partition_broadcast(GEN_EDGES)).then_inc(step_landed, 16)
                    sp.dma_start(dst_own[:], dst[edges].rearrange("(e a) -> e a", a=1)).then_inc(step_landed, 16)
                    sp.dma_start(src_own[:], src[edges].rearrange("(e a) -> e a", a=1)).then_inc(step_landed, 16)
                sp.wait_ge(added, GEN_STEPS * 16 + 16)
                sp.sem_inc(result_done, 1)
                with sp.Fori(0, GEN_TILES, 1) as n:
                    nodes = bass.ds(n * GEN_ROWS, GEN_ROWS)
                    sp.wait_ge(result_done, n + 1)
                    sp.dma_start(x_rows[:], x[nodes, :]).then_inc(tile_landed, 16)
                    sp.dma_start(sum_rows[:], sums_dram[nodes, :]).then_inc(tile_landed, 16)

            only_if_needed(sp, program)

        @block.gpsimd
        def _(pool):
            def program(pool):
                pool.wait_ge(zeroed, 16 * (SUM_ROWS // (P * ZERO_ROWS)))
                with pool.Fori(0, GEN_STEPS, 1) as s:
                    pool.wait_ge(step_landed, s * 48 + 48)
                    pool.sem_inc(rows_wanted, 1)
                    nc.gpsimd.indirect_dma_start(rows[:, 0:DIM], None, x,
                                                 bass.IndirectOffsetOnAxis(ap=src_own[:, 0:1], axis=0)).then_inc(rows_landed, 16)
                    pool.wait_ge(target_done, s + 1)
                    pool.wait_ge(totals_copied, s + 1)
                    pool.sem_inc(adds_wanted, 1)
                    nc.gpsimd.indirect_dma_start(sums_dram, bass.IndirectOffsetOnAxis(ap=target[:, 0:1], axis=0), totals[:], None,
                                                 compute_op=ALU.add).then_inc(added, 16)

            only_if_needed(pool, program)

        @block.vector
        def _(dve):
            def program(dve):
                v = nc.vector
                v.memset(zero_rows[:], 0.0).then_inc(zeros_set, 1)
                v.memset(rows[:, DIM:DIM + 1], 1.0)
                v.memset(rows[:, DIM + 1:ROW], 0.0)
                v.tensor_scalar(spare_row[:], k.partition[0:GEN_EDGES, :], float(NODES), None, ALU.add)
                v.tensor_scalar(earlier[:], k.column[0:GEN_EDGES, 0:GEN_EDGES], k.partition[0:GEN_EDGES, 0:1], None, ALU.is_lt).then_inc(zeros_set, 1)
                dve.wait_ge(zeros_set, 2)
                with dve.Fori(0, GEN_STEPS, 1) as s:
                    links = [0]

                    def link(ins):
                        links[0] += 1
                        ins.then_inc(order, 1)
                        dve.wait_ge(order, s * EDGE_LINKS + links[0])

                    dve.wait_ge(step_landed, s * 48 + 48)
                    link(v.tensor_copy(dst_value[:], dst_own[:]))
                    v.tensor_scalar(same[:], dst_line[:], dst_value[:, 0:1], None, ALU.is_equal).then_inc(same_done, 1)
                    dve.wait_ge(same_done, s + 1)
                    link(v.tensor_tensor(same_earlier[:], same[:], earlier[:], ALU.mult))
                    link(v.reduce_sum(repeats[:], same_earlier[:], AXIS_X))
                    link(v.tensor_scalar(is_repeat[:], repeats[:], 0.0, None, ALU.is_gt))
                    link(v.tensor_tensor(to_spare[:], spare_row[:], dst_value[:], ALU.subtract))
                    link(v.tensor_tensor(moved[:], to_spare[:], is_repeat[:], ALU.mult))
                    link(v.tensor_tensor(moved[:], moved[:], dst_value[:], ALU.add))
                    v.tensor_copy(target[:], moved[:]).then_inc(target_done, 1)
                    dve.wait_ge(target_done, s + 1)
                    dve.wait_ge(totals_done, s + 1)
                    link(v.tensor_copy(totals[:, 0:DIM], totals_bank[0:GEN_EDGES, 0:DIM]))
                    link(v.tensor_copy(totals[:, DIM:ROW], totals_bank[0:GEN_EDGES, DIM:ROW]))
                    dve.sem_inc(totals_copied, 1)
                dve.wait_ge(bs_landed, 16)
                dve.sem_inc(stored, 16)
                with dve.Fori(0, GEN_TILES, 1) as n:
                    links = [0]

                    def link(ins):
                        links[0] += 1
                        ins.then_inc(order, 1)
                        dve.wait_ge(order, n * TILE_LINKS + (GEN_STEPS * EDGE_LINKS + links[0]))

                    dve.wait_ge(h_done, n + 1)
                    link(v.tensor_tensor(biased[:], bs[0:GEN_ROWS, :], h_bank[0:GEN_ROWS, 0:DIM], ALU.add))
                    link(v.scalar_tensor_tensor(before_relu[:], k.bn[0:GEN_ROWS, :], sum_rows[:, DIM:DIM + 1], biased[:], ALU.mult, ALU.add))
                    link(v.scalar_tensor_tensor(y[:], before_relu[:], 0.0, x_rows[:], ALU.max, ALU.add))
                    link(v.bn_stats(stats[:], y[:]))
                    dve.sem_inc(zeros_set, 1)
                    v.bn_aggr(mean_var[:], stats[:]).then_inc(var_done, 1)
                    dve.wait_ge(std_done, n + 1)
                    link(v.reciprocal(rstd[:], std[:]))
                    dve.wait_ge(stored, n * 16 + 16)
                    v.tensor_scalar(result[:], y[:], mean_var[:, 0:1], rstd[:, 0:1], ALU.subtract, ALU.mult).then_inc(result_done, 1)

            only_if_needed(dve, program)

        @block.tensor
        def _(pe):
            def program(pe):
                mm = nc.tensor.matmul
                pe.wait_ge(zeros_set, 2)
                with pe.Fori(0, GEN_STEPS, 1) as s:
                    pe.wait_ge(same_done, s + 1)
                    pe.wait_ge(rows_landed, s * 16 + 16)
                    mm(totals_bank[0:GEN_EDGES, 0:ROW], same[:], rows[:], start=True, stop=True).then_inc(totals_done, 1)
                with pe.Fori(0, GEN_TILES, 1) as n:
                    pe.wait_ge(tile_landed, n * 32 + 32)
                    nc.tensor.transpose(turn_bank[:, 0:GEN_ROWS], x_rows[:], k.identity[0:GEN_ROWS, 0:GEN_ROWS])
                    nc.tensor.transpose(turn_bank[:, GEN_ROWS:2 * GEN_ROWS], sum_rows[:, 0:DIM],
                                        k.identity[0:GEN_ROWS, 0:GEN_ROWS]).then_inc(turned, 1)
                    pe.wait_ge(turned_copied, n + 1)
                    mm(h_bank[0:GEN_ROWS, 0:DIM], x_turned[:, 0, :], k.ws_t[:], start=True, stop=False)
                    mm(h_bank[0:GEN_ROWS, 0:DIM], x_turned[:, 1, :], k.wn_t[:], start=False, stop=True).then_inc(h_done, 1)

            only_if_needed(pe, program)

        @block.scalar
        def _(act):
            def program(act):
                with act.Fori(0, GEN_TILES, 1) as n:
                    act.wait_ge(turned, n + 1)
                    nc.scalar.copy(x_turned[:], turn_bank[:, 0:2 * GEN_ROWS].rearrange("p (a r) -> p a r", a=2)).then_inc(turned_copied, 1)
                    act.wait_ge(var_done, n + 1)
                    nc.scalar.activation(std[:], mean_var[:, 1:2], ACT.Sqrt, bias=k.eps[0:GEN_ROWS, 0:1], scale=1.0).then_inc(std_done, 1)
                    act.wait_ge(result_done, n + 2)
                    act.dma_start(out[bass.ds(n * GEN_ROWS, GEN_ROWS), :], result[:]).then_inc(stored, 16)
                act.wait_ge(stored, GEN_TILES * 16 + 16)

            only_if_needed(act, program)


INPUTS = ["x", "src", "dst", "L0_gnn_W_self", "L0_gnn_b_self", "L0_gnn_W_neigh", "L0_gnn_b_neigh"]


def kernel(**inputs):
    import concourse.bacc as bacc
    from concourse.bass_utils import run_bass_kernel_spmd

    nc = bacc.Bacc("TRN2", target_bir_lowering=False, num_devices=1)
    arrays, args = {}, []
    for name in INPUTS:
        a = np.ascontiguousarray(inputs[name])
        arrays[f"in_{name}"] = a
        args.append(nc.dram_tensor(f"in_{name}", a.shape, mybir.dt.from_np(a.dtype), kind="ExternalInput").ap())
    out = nc.dram_tensor("out", (NODES, DIM), FP32, kind="ExternalOutput").ap()
    gnn_kernel(nc, *args, out)
    done = run_bass_kernel_spmd(nc, [arrays], core_ids=[0])
    return done.results[0]["out"]
```

```python
import numpy as np

import concourse.bass as bass
from concourse import mybir
from contextlib import ExitStack

FP32 = mybir.dt.float32
BF16 = mybir.dt.bfloat16
INT32 = mybir.dt.int32
ALU = mybir.AluOpType
ACT = mybir.ActivationFunctionType
AXIS_X = mybir.AxisListType.X

P = 128
NODES, DIM, EDGES = 50000, 128, 100000
EPS = 1e-5

EDGE_ROWS = 125
EDGE_COLS = EDGES // EDGE_ROWS
BLOCK = 200
BLOCKS = EDGES // BLOCK
BLOCKS_PER_ROW = EDGE_COLS // BLOCK

TILES = -(-NODES // P)
LAST_ROWS = NODES - (TILES - 1) * P
PACKED = EDGES - NODES
CHUNKS = -(-PACKED // P)
COLUMNS = 4
SPREAD = -(-(CHUNKS + 1) // COLUMNS)
ENTRIES = SPREAD * COLUMNS

WINDOW = 312
SHIFT_BITS = 8
HIGH_BITS = -(1 << 16)
PAD = 400
NO_NODE = 65535

SPAN = 3
DRIFT = 8
RING = 96
STAGE = 16
GATHER_SEMS = 12
ROW = DIM + 4
TABLE = SPAN + 1

TRIO = 3
TRIOS = -(-TILES // TRIO)
TRIO_TABLE = TRIO * TABLE + 1
DEEP = 4

LOOPED = ((CHUNKS - DRIFT - SPAN) // TRIO - 1) // DEEP * DEEP

GEN_EDGES = 125
GEN_STEPS = EDGES // GEN_EDGES
GEN_ROWS = 125
GEN_TILES = NODES // GEN_ROWS
ZERO_ROWS = 28
SUM_ROWS = 14 * P * ZERO_ROWS


def gnn_kernel(nc, x, src, dst, w_self, b_self, w_neigh, b_neigh, out):
    with ExitStack() as ctx:
        def sb(name, shape, dtype=FP32):
            return ctx.enter_context(nc.sbuf_tensor(name, shape, dtype))

        def sem(name):
            return ctx.enter_context(nc.semaphore(name))

        weights = build_constants(nc, sb, sem, w_self, b_self, w_neigh, b_neigh)
        with ExitStack() as fast:
            build_common_case(nc, fast, weights, x, src, dst, out)
        with ExitStack() as general:
            build_general_case(nc, general, weights, x, src, dst, out)


class Constants:
    pass


def build_constants(nc, sb, sem, w_self, b_self, w_neigh, b_neigh):
    k = Constants()
    k.column = sb("column", [P, P])
    k.partition = sb("partition", [P, 1])
    k.identity = sb("identity", [P, P])
    k.before = sb("before", [P, P])
    k.ones_bf = sb("ones_bf", [P, P], BF16)
    k.ones = sb("ones", [P, P])
    k.eps = sb("eps", [P, 1])
    k.ws = sb("ws", [P, DIM])
    k.wn = sb("wn", [P, DIM])
    k.wsum = sb("wsum", [P, DIM])
    k.ws_t = sb("ws_t", [P, DIM])
    k.wn_t = sb("wn_t", [P, DIM])
    k.wsum_t = sb("wsum_t", [P, DIM])
    k.bn = sb("bn", [P, DIM])
    k.bs_row = sb("bs_row", [1, DIM])
    k.bn_row = sb("bn_row", [1, DIM])
    k.bsn_row = sb("bsn_row", [1, DIM])
    k.bsn_rest = sb("bsn_rest", [1, 2, DIM])
    k.bsn_part = sb("bsn_part", [1, 3, DIM], BF16)
    k.bsn3 = sb("bsn3", [3, DIM], BF16)
    k.needs_general = sb("needs_general", [1, 1], INT32)
    return_sems(k, sem)
    k.inputs = (w_self, b_self, w_neigh, b_neigh)
    return k


def return_sems(k, sem):
    k.iotas = sem("iotas")
    k.weights_landed = sem("weights_landed")
    k.bn_landed = sem("bn_landed")
    k.consts_made = sem("consts_made")
    k.weights_turned = sem("weights_turned")
    k.weights_copied = sem("weights_copied")
    k.parts_made = sem("parts_made")
    k.parts_landed = sem("parts_landed")


def build_common_case(nc, ctx, k, x, src, dst, out):
    def sb(name, shape, dtype=FP32):
        return ctx.enter_context(nc.sbuf_tensor(name, shape, dtype))

    def sem(name):
        return ctx.enter_context(nc.semaphore(name))

    def scratch(name, shape, dtype):
        return nc.dram_tensor(name, shape, dtype, kind="Internal").ap()

    w_self, b_self, w_neigh, b_neigh = k.inputs

    words_padded = scratch("words_padded", (EDGES + PAD, 1), INT32)
    kept_upto_dram = scratch("kept_upto_dram", (BLOCKS, BLOCK), FP32)
    ends_dram = scratch("ends_dram", (1, EDGE_ROWS * 2 * BLOCKS_PER_ROW), FP32)
    table_dram = scratch("table_dram", (ENTRIES, TABLE), INT32)
    bounds_dram = scratch("bounds_dram", (ENTRIES, 3), FP32)

    edge_src = sb("edge_src", [EDGE_ROWS, EDGE_COLS], INT32)
    edge_dst = sb("edge_dst", [EDGE_ROWS, EDGE_COLS + 1], INT32)
    flag_a = sb("flag_a", [EDGE_ROWS, EDGE_COLS])
    flag_b = sb("flag_b", [EDGE_ROWS, EDGE_COLS])
    zeros = sb("zeros", [EDGE_ROWS, EDGE_COLS])
    kept_upto = sb("kept_upto", [EDGE_ROWS, EDGE_COLS])
    dst_if_kept = sb("dst_if_kept", [EDGE_ROWS, EDGE_COLS], INT32)
    edge_words = sb("edge_words", [EDGE_ROWS, EDGE_COLS], INT32)
    pad_words = sb("pad_words", [1, PAD], INT32)
    rows_before = sb("rows_before", [EDGE_ROWS, 1])
    ends = sb("ends", [EDGE_ROWS, 2, BLOCKS_PER_ROW])
    all_ends = sb("all_ends", [SPREAD, EDGE_ROWS, 2, BLOCKS_PER_ROW])
    below = [sb(f"below{j}", [SPREAD, EDGE_ROWS * BLOCKS_PER_ROW]) for j in range(COLUMNS)]
    laps = [sb(f"laps{i}", [SPREAD, SPAN, COLUMNS]) for i in range(2)]
    drift_out = sb("drift_out", [SPREAD, COLUMNS])
    limit = sb("limit", [SPREAD, COLUMNS])
    entry = sb("entry", [SPREAD, COLUMNS])
    counts = sb("counts", [SPREAD, 2, COLUMNS])
    block = sb("block", [SPREAD, 2, COLUMNS])
    block_index = sb("block_index", [SPREAD, 2, COLUMNS], INT32)
    in_block = sb("in_block", [SPREAD, 2, COLUMNS])
    kept_block = sb("kept_block", [SPREAD, COLUMNS, BLOCK])
    dst_block = sb("dst_block", [SPREAD, COLUMNS, BLOCK], INT32)
    place = sb("place", [SPREAD, 2, COLUMNS])
    place_index = sb("place_index", [SPREAD, 2, COLUMNS], INT32)
    packed_before = sb("packed_before", [SPREAD, COLUMNS])
    first_int = sb("first_int", [SPREAD, COLUMNS], INT32)
    drift = sb("drift", [SPREAD, COLUMNS])
    drift_in = sb("drift_in", [SPREAD, COLUMNS])
    first = sb("first", [SPREAD, COLUMNS])
    ring_slot = sb("ring_slot", [SPREAD, SPAN, COLUMNS])
    table = sb("table", [SPREAD, COLUMNS, TABLE], INT32)
    table_row = sb("table_row", [1, TRIOS, TRIO_TABLE], INT32)
    bounds = sb("bounds", [SPREAD, COLUMNS, 3])
    bounds_row = sb("bounds_row", [1, ENTRIES, 3])
    cover = sb("cover", [1, TILES])
    length = sb("length", [1, CHUNKS])
    too_long = sb("too_long", [1, CHUNKS])
    thirds = sb("thirds", [1, TRIOS * TRIO])
    trio_thirds = sb("trio_thirds", [1, TRIOS])
    checks = sb("checks", [P, 6])
    check_sums = sb("check_sums", [1, 6])
    check_all = sb("check_all", [1, 3])

    window = [sb(f"window{i}", [SPREAD, COLUMNS, WINDOW], INT32) for i in range(2)]
    low = sb("low", [SPREAD, COLUMNS, WINDOW], INT32)
    moves = sb("moves", [SPREAD, COLUMNS, WINDOW], INT32)
    first_dst = sb("first_dst", [SPREAD, COLUMNS])
    pair_field = sb("pair_field", [SPREAD, 2, COLUMNS, P], INT32)
    pair_value = sb("pair_value", [SPREAD, 2, COLUMNS, P])
    chunk_src = sb("chunk_src", [P, ENTRIES], INT32)
    chunk_dst = sb("chunk_dst", [P, ENTRIES + 1])

    column3 = sb("column3", [P, SPAN, P])
    tile_base = sb("tile_base", [P, TILES])
    staged = sb("staged", [P, RING], INT32)
    ring = sb("ring", [P, RING, ROW])
    x_in = [sb(f"x_in{i}", [P, TRIO, DIM]) for i in range(DEEP)]
    pick = [sb(f"pick{i}", [P, TRIO, SPAN, P]) for i in range(2)]
    sums = [sb(f"sums{i}", [P, TRIO, ROW]) for i in range(DEEP)]
    x_t = [sb(f"x_t{i}", [P, TRIO, P]) for i in range(2)]
    sums_t = [sb(f"sums_t{i}", [P, TRIO, P]) for i in range(2)]
    with_degree = [sb(f"with_degree{i}", [P, TRIO, DIM]) for i in range(2)]
    y = [sb(f"y{i}", [P, TRIO, DIM]) for i in range(DEEP)]
    stats = [sb(f"stats{i}", [P, TRIO, 6]) for i in range(DEEP)]
    mean_var = [sb(f"mean_var{i}", [P, TRIO, 2]) for i in range(DEEP)]
    std = [sb(f"std{i}", [P, TRIO]) for i in range(DEEP)]
    rstd = [sb(f"rstd{i}", [P, TRIO]) for i in range(DEEP)]
    minus_mean = [sb(f"minus_mean{i}", [P, TRIO]) for i in range(DEEP)]
    result = [sb(f"result{i}", [P, TRIO, DIM]) for i in range(DEEP)]

    bank = [ctx.enter_context(nc.psum_tensor(f"bank{i}", [P, 512], FP32)) for i in range(8)]
    sum_bank, xt_bank, st_bank, h_bank = bank[0:2], bank[2:4], bank[4:6], bank[6:8]

    edges_landed = sem("edges_landed")
    next_landed = sem("next_landed")
    next_set = sem("next_set")
    pads_set = sem("pads_set")
    padded_stored = sem("padded_stored")
    row_counts = sem("row_counts")
    rows_summed = sem("rows_summed")
    upto_done = sem("upto_done")
    upto_stored = sem("upto_stored")
    ends_done = sem("ends_done")
    ends_stored = sem("ends_stored")
    ends_landed = sem("ends_landed")
    blocks_found = sem("blocks_found")
    block_landed = [sem(f"block_landed{i}") for i in range(2 * COLUMNS)]
    places_found = sem("places_found")
    window_landed = [sem(f"window_landed{i}") for i in range(COLUMNS)]
    table_done = sem("table_done")
    table_stored = sem("table_stored")
    table_landed = sem("table_landed")
    thirds_done = sem("thirds_done")
    words_done = sem("words_done")
    fields_done = sem("fields_done")
    fields_turned = sem("fields_turned")
    chunks_known = sem("chunks_known")
    dve_order = sem("dve_order")
    checks_done = sem("checks_done")
    checks_summed = sem("checks_summed")
    gathered = [sem(f"gathered{i}") for i in range(GATHER_SEMS)]
    stage_done = sem("stage_done")
    slots_free = sem("slots_free")
    ones_set = sem("ones_set")
    x_landed = [sem(f"x_landed{i}") for i in range(DEEP)]
    pick_built = sem("pick_built")
    tiles_summed = sem("tiles_summed")
    sums_copied = sem("sums_copied")
    st_turned = sem("st_turned")
    st_copied = sem("st_copied")
    xt_turned = sem("xt_turned")
    xt_copied = sem("xt_copied")
    h_done = sem("h_done")
    h_used = sem("h_used")
    y_done = sem("y_done")
    stats_done = sem("stats_done")
    mean_var_done = sem("mean_var_done")
    std_done = sem("std_done")
    rstd_done = sem("rstd_done")
    norm_ready = sem("norm_ready")
    result_done = sem("result_done")
    stored = [sem(f"stored{i}") for i in range(DEEP)]

    def tiles_of(tau):
        return (1, LAST_ROWS) if isinstance(tau, int) and tau == TRIOS - 1 else (TRIO, P)

    def rows_of(dram, tau):
        tiles, rows = tiles_of(tau)
        if tiles == 1:
            return dram[NODES - rows:NODES, :].rearrange("(t p) d -> p t d", t=1)
        return dram[bass.ds(tau * (TRIO * P), TRIO * P), :].rearrange("(t p) d -> p t d", t=TRIO)


    def load_table(engine, tau, tiles):
        registers = [engine.alloc_register(nc.get_next_instruction_name().replace("I-", "word")) for _ in range(TRIO_TABLE)]
        engine.load(registers, table_row[:].rearrange("a e w -> a (e w)")[:, bass.ds(tau * TRIO_TABLE, TRIO_TABLE)])
        return [registers[q * TABLE:(q + 1) * TABLE] for q in range(TRIO)] + [registers[-1:]]

    def free_table(engine, table_registers):
        for register in sum(table_registers, []):
            engine.free_register(register)

    with nc.Block() as block_:
        @block_.sync
        def _(sp):
            sp.dma_start(edge_src[:], src.rearrange("(p e) -> p e", p=EDGE_ROWS)).then_inc(edges_landed, 16)
            sp.dma_start(edge_dst[:, 0:EDGE_COLS], dst.rearrange("(p e) -> p e", p=EDGE_ROWS)).then_inc(edges_landed, 16)
            sp.wait_ge(next_set, 1)
            sp.dma_start(edge_dst[0:EDGE_ROWS - 1, EDGE_COLS:EDGE_COLS + 1],
                         dst.rearrange("(p e) -> p e", p=EDGE_ROWS)[1:EDGE_ROWS, 0:1],
                         allow_slow_non_contiguous=True).then_inc(next_landed, 16)
            sp.dma_start(k.ws[:], w_self).then_inc(k.weights_landed, 16)
            sp.dma_start(k.wn[:], w_neigh).then_inc(k.weights_landed, 16)
            sp.dma_start(k.bs_row[:], b_self.rearrange("(a d) -> a d", a=1)).then_inc(k.weights_landed, 16)
            sp.dma_start(k.bn_row[:], b_neigh.rearrange("(a d) -> a d", a=1)).then_inc(k.weights_landed, 16)
            sp.dma_start(k.bn[:], b_neigh.rearrange("(a d) -> a d", a=1).partition_broadcast(P)).then_inc(k.bn_landed, 16)
            sp.wait_ge(pads_set, 1)
            sp.dma_start(words_padded[EDGES:EDGES + PAD, :].rearrange("e o -> o e"), pad_words[:]).then_inc(padded_stored, 16)
            for tau in range(DEEP):
                sp.dma_start(x_in[tau][:], rows_of(x, tau)).then_inc(x_landed[tau], 16)
            sp.wait_ge(ends_done, 1)
            sp.dma_start(ends_dram[0, :].rearrange("(p w) -> p w", p=EDGE_ROWS), ends[:].rearrange("p a b -> p (a b)")).then_inc(ends_stored, 16)
            sp.wait_ge(upto_done, 1)
            sp.dma_start(kept_upto_dram.rearrange("(p b) e -> p (b e)", p=EDGE_ROWS), kept_upto[:]).then_inc(upto_stored, 16)
            sp.wait_ge(ends_stored, 16)
            sp.dma_start(all_ends[:].rearrange("p a b c -> p (a b c)"), ends_dram.partition_broadcast(SPREAD)).then_inc(ends_landed, 16)
            sp.wait_ge(words_done, 1)
            sp.dma_start(words_padded[0:EDGES, :].rearrange("(p e) o -> p (e o)", p=EDGE_ROWS), edge_words[:]).then_inc(padded_stored, 16)
            sp.wait_ge(k.parts_made, 3)
            sp.dma_start(k.bsn3[:], k.bsn_part[:]).then_inc(k.parts_landed, 16)
            sp.wait_ge(table_done, 1)
            for mine, dram in ((table, table_dram), (bounds, bounds_dram)):
                sp.dma_start(dram.rearrange("(j p) w -> p j w", p=SPREAD), mine[:]).then_inc(table_stored, 16)
            sp.wait_ge(table_stored, 32)
            sp.dma_start(bounds_row[:].rearrange("a e w -> a (e w)"),
                         bounds_dram.rearrange("e w -> (e w)").rearrange("(a w) -> a w", a=1)).then_inc(table_landed, 16)
            whole = TILES // TRIO * TRIO
            sp.dma_start(table_row[:, 0:whole // TRIO, 0:TRIO * TABLE],
                         table_dram[0:whole, :].rearrange("(a n q) w -> a n (q w)", a=1, q=TRIO)).then_inc(table_landed, 16)
            sp.wait_ge(next_set, 2)
            sp.dma_start(table_row[:, whole // TRIO, 0:(TILES - whole) * TABLE],
                         table_dram[whole:TILES, :].rearrange("(a q) w -> a (q w)", a=1)).then_inc(table_landed, 16)

            def load_x(t, u):
                tau = t + u
                sp.wait_ge(y_done, tau - DEEP + 1)
                sp.dma_start(x_in[u % DEEP][0:tiles_of(tau)[1], 0:tiles_of(tau)[0], :], rows_of(x, tau)).then_inc(x_landed[u % DEEP], 16)

            def store(t, u):
                tau = t + u
                tiles, rows = tiles_of(tau)
                sp.wait_ge(result_done, tau + 1)
                sp.dma_start(rows_of(out, tau), result[u % DEEP][0:rows, 0:tiles, :]).then_inc(stored[u % DEEP], 16)

            def step(t, u):
                tau = t + u
                known = isinstance(tau, int)
                if not known or tau < TRIOS:
                    load_x(t, u)
                if not known or tau >= DEEP + 2:
                    store(t, u - DEEP - 2)

            for u in range(DEEP):
                step(DEEP, u)
            with sp.Fori(2 * DEEP, LOOPED - DEEP + 1, DEEP) as t:
                for u in range(DEEP):
                    step(t, u)
            for u in range(TRIOS + DEEP + 2 - LOOPED):
                step(LOOPED, u)
            for i in range(DEEP):
                sp.wait_ge(stored[i], 16 * len(range(i, TRIOS, DEEP)))

        @block_.gpsimd
        def _(pool):
            def iota(out_, pattern, multiplier):
                return nc.gpsimd.iota(out_, pattern, base=0, channel_multiplier=multiplier, allow_small_or_imprecise_dtypes=True)

            iota(k.column[:], [[1, P]], 0).then_inc(k.iotas, 1)
            iota(k.partition[:], [[1, 1]], 1).then_inc(k.iotas, 1)
            iota(limit[:], [[P * SPREAD, COLUMNS]], P).then_inc(k.iotas, 1)
            iota(entry[:], [[SPREAD, COLUMNS]], 1).then_inc(k.iotas, 1)
            iota(column3[:], [[0, SPAN], [1, P]], 0).then_inc(k.iotas, 1)
            iota(tile_base[:], [[P, TILES]], 0).then_inc(k.iotas, 1)
            nc.gpsimd.memset(ring[:, :, DIM:DIM + 1], 1.0).then_inc(ones_set, 1)
            pool.wait_ge(upto_stored, 16)
            for a in range(2):
                for j in range(COLUMNS):
                    pool.wait_ge(blocks_found, a + 1)
                    if a == 0:
                        nc.gpsimd.indirect_dma_start(kept_block[:, j, :], None, kept_upto_dram,
                                                     bass.IndirectOffsetOnAxis(ap=block_index[:, a, j:j + 1], axis=0)
                                                     ).then_inc(block_landed[j], 16)
                    else:
                        nc.gpsimd.indirect_dma_start(dst_block[:, j, :], None, dst.rearrange("(b e) -> b e", e=BLOCK),
                                                     bass.IndirectOffsetOnAxis(ap=block_index[:, a, j:j + 1], axis=0)
                                                     ).then_inc(block_landed[COLUMNS + j], 16)
            pool.wait_ge(padded_stored, 32)
            pool.wait_ge(places_found, 1)
            for j in range(COLUMNS):
                nc.gpsimd.indirect_dma_start(window[0][:, j, :], None, words_padded,
                                             bass.IndirectOffsetOnAxis(ap=place_index[:, 0, j:j + 1], axis=0)
                                             ).then_inc(window_landed[j], 16)

            def gather(r, slot):
                round_ = slot // GATHER_SEMS
                if not (isinstance(r, int) and r == 0 and round_ == 0):
                    pool.wait_ge(gathered[slot % GATHER_SEMS], r * (16 * (RING // GATHER_SEMS)) + 16 * round_)
                    pool.sem_inc(slots_free, 1)
                nc.gpsimd.indirect_dma_start(ring[:, slot, 0:DIM], None, x,
                                             bass.IndirectOffsetOnAxis(ap=staged[:, slot:slot + 1], axis=0)
                                             ).then_inc(gathered[slot % GATHER_SEMS], 16)

            def stage(r, h, count):
                if not (isinstance(r, int) and r == 0):
                    pool.wait_ge(tiles_summed, r * RING + (h * STAGE + STAGE - 1 - RING + DRIFT + 1))
                nc.gpsimd.tensor_copy(staged[:, h * STAGE:h * STAGE + count],
                                      chunk_src[:, bass.ds(r * RING + h * STAGE, count)]).then_inc(stage_done, 1)
                pool.wait_ge(stage_done, r * (RING // STAGE) + h + 1)
                for slot in range(h * STAGE, h * STAGE + count):
                    gather(r, slot)

            pool.wait_ge(chunks_known, 2)
            for h in range(RING // STAGE):
                stage(0, h, STAGE)
            pool.wait_ge(chunks_known, 4)
            with pool.Fori(1, CHUNKS // RING, 1) as r:
                for h in range(RING // STAGE):
                    stage(r, h, STAGE)
            stage(CHUNKS // RING, 0, CHUNKS % RING)

        @block_.vector
        def _(dve):
            chain = [0]

            def link(ins):
                chain[0] += 1
                ins.then_inc(dve_order, 1)
                dve.wait_ge(dve_order, chain[0])

            v = nc.vector
            v.memset(edge_dst[:, EDGE_COLS:EDGE_COLS + 1], NO_NODE).then_inc(next_set, 1)
            v.memset(pad_words[:], NODES).then_inc(pads_set, 1)
            v.memset(table_row[:, TRIOS - 1:TRIOS, :], 0).then_inc(next_set, 1)
            v.memset(thirds[:], 0.0)
            v.memset(k.ones[:], 1.0)
            v.memset(k.eps[:], EPS)
            v.memset(zeros[:], 0.0)
            v.memset(checks[:], 0.0)
            v.memset(chunk_dst[:, ENTRIES:ENTRIES + 1], float(NO_NODE))
            link(v.memset(k.ones_bf[:], 1.0))
            dve.wait_ge(k.iotas, 2)
            v.tensor_scalar(k.before[:], k.column[:], k.partition[:, 0:1], None, ALU.is_gt)
            v.tensor_scalar(k.identity[:], k.column[:], k.partition[:, 0:1], None, ALU.is_equal).then_inc(k.consts_made, 1)

            dve.wait_ge(edges_landed, 32)
            v.tensor_tensor(flag_a[:], edge_src[:], edge_dst[:, 0:EDGE_COLS], ALU.is_equal)
            dve.wait_ge(next_landed, 16)
            link(v.tensor_tensor(flag_b[:], edge_dst[:, 1:EDGE_COLS + 1], edge_dst[:, 0:EDGE_COLS], ALU.not_equal))
            link(v.tensor_tensor(flag_a[:], flag_a[:], flag_b[:], ALU.mult))
            link(v.tensor_scalar(flag_b[:], flag_a[:], -1.0, 1.0, ALU.mult, ALU.add))
            v.tensor_tensor_scan(kept_upto[:], flag_b[:], zeros[:], 0.0, ALU.add, ALU.add).then_inc(row_counts, 1)
            dve.wait_ge(rows_summed, 1)
            link(v.tensor_copy(rows_before[:], bank[0][0:EDGE_ROWS, 0:1]))
            link(v.tensor_copy(checks[0:EDGE_ROWS, 4:5], kept_upto[:, EDGE_COLS - 1:EDGE_COLS]))
            v.tensor_scalar(kept_upto[:], kept_upto[:], rows_before[:, 0:1], None, ALU.add).then_inc(upto_done, 1)
            dve.wait_ge(upto_done, 1)
            v.tensor_copy(ends[:, 0, :], kept_upto[:, BLOCK - 1:EDGE_COLS:BLOCK])
            v.tensor_copy(ends[:, 1, :], edge_dst[:, BLOCK - 1:EDGE_COLS:BLOCK]).then_inc(ends_done, 1)
            link(v.tensor_tensor(dst_if_kept[:], edge_dst[:, 0:EDGE_COLS], flag_b[:], ALU.mult))
            v.scalar_tensor_tensor(edge_words[:], edge_src[:], 16, dst_if_kept[:], ALU.logical_shift_left, ALU.bitwise_or).then_inc(words_done, 1)
            dve.wait_ge(k.weights_landed, 64)
            v.tensor_tensor(k.wsum[:], k.ws[:], k.wn[:], ALU.add).then_inc(k.consts_made, 1)
            link(v.tensor_tensor(k.bsn_row[:], k.bs_row[:], k.bn_row[:], ALU.add))
            v.tensor_copy(k.bsn_part[:, 0, :], k.bsn_row[:]).then_inc(k.parts_made, 1)
            dve.wait_ge(k.parts_made, 1)
            link(v.tensor_tensor(k.bsn_rest[:, 0, :], k.bsn_row[:], k.bsn_part[:, 0, :], ALU.subtract))
            v.tensor_copy(k.bsn_part[:, 1, :], k.bsn_rest[:, 0, :]).then_inc(k.parts_made, 1)
            dve.wait_ge(k.parts_made, 2)
            link(v.tensor_tensor(k.bsn_rest[:, 1, :], k.bsn_rest[:, 0, :], k.bsn_part[:, 1, :], ALU.subtract))
            v.tensor_copy(k.bsn_part[:, 2, :], k.bsn_rest[:, 1, :]).then_inc(k.parts_made, 1)

            dve.wait_ge(ends_landed, 16)
            dve.wait_ge(k.iotas, 6)
            for a, less in ((0, ALU.is_le), (1, ALU.is_lt)):
                for j in range(COLUMNS):
                    ins = v.tensor_scalar(below[j][:].rearrange("p (a b) -> p a b", a=EDGE_ROWS), all_ends[:, :, a, :],
                                          limit[:, j:j + 1], 0.0, less, ALU.add, accum_out=counts[:, a, j:j + 1])
                link(ins)
                link(v.tensor_scalar(block[:, a, :], counts[:, a, :], float(BLOCKS - 1), None, ALU.min))
                v.tensor_copy(block_index[:, a, :], block[:, a, :]).then_inc(blocks_found, 1)
            def find_places(a):
                blocks_, less = ((kept_block, ALU.is_le), (dst_block, ALU.is_lt))[a]
                for j in range(COLUMNS):
                    dve.wait_ge(block_landed[a * COLUMNS + j], 16)
                    ins = v.tensor_scalar(below[j][:, 0:BLOCK], blocks_[:, j, :], limit[:, j:j + 1], 0.0, less, ALU.add,
                                          accum_out=in_block[:, a, j:j + 1])
                link(ins)
                link(v.scalar_tensor_tensor(place[:, a, :], block[:, a, :], float(BLOCK), in_block[:, a, :], ALU.mult, ALU.add))
                v.tensor_copy(place_index[:, a, :], place[:, a, :]).then_inc(places_found, 1)

            find_places(0)
            find_places(1)

            link(v.tensor_tensor(packed_before[:], place[:, 1, :], limit[:], ALU.subtract))
            dve.wait_ge(places_found, 2)
            link(v.tensor_scalar(first_int[:], place_index[:, 1, :], 7, None, ALU.logical_shift_right))
            link(v.tensor_copy(first[:], first_int[:]))
            link(v.tensor_tensor(first[:], first[:], entry[:], ALU.subtract))
            link(v.tensor_tensor(drift[:], first[:], entry[:], ALU.subtract))
            link(v.tensor_scalar(drift_in[:], drift[:], float(-DRIFT), float(DRIFT), ALU.max, ALU.min))
            link(v.tensor_tensor(first[:], drift_in[:], entry[:], ALU.add))
            link(v.tensor_scalar(first[:], first[:], 0.0, float(CHUNKS - 1), ALU.max, ALU.min))
            for s in range(SPAN):
                link(v.tensor_scalar(ring_slot[:, s, :], first[:], float(s), None, ALU.add))
            link(v.tensor_scalar(laps[1][:], ring_slot[:], float(RING), None, ALU.is_ge))
            top = (CHUNKS + SPAN) // RING
            for lap in range(2, top + 1):
                link(v.scalar_tensor_tensor(laps[lap % 2][:], ring_slot[:], float(RING * lap), laps[1 - lap % 2][:], ALU.is_ge, ALU.add))
            link(v.scalar_tensor_tensor(ring_slot[:], laps[top % 2][:], float(-RING), ring_slot[:], ALU.mult, ALU.add))
            for s in range(SPAN):
                v.tensor_scalar(table[:, :, s], ring_slot[:, s, :], float(ROW), None, ALU.mult)
            v.tensor_copy(table[:, :, SPAN], first[:])
            v.tensor_copy(bounds[:, :, 0], packed_before[:])
            v.tensor_copy(bounds[:, :, 2], place[:, 0, :])
            v.tensor_scalar(bounds[:, :, 1], first[:], float(P), float((SPAN - 1) * P), ALU.mult, ALU.add).then_inc(table_done, 1)

            def pack(j0, j1):
                js = slice(j0, j1)
                for j in range(j0, j1):
                    dve.wait_ge(window_landed[j], 16)
                link(v.tensor_scalar(low[:, js, :], window[0][:, js, :], 0xFFFF, None, ALU.bitwise_and))
                link(v.tensor_copy(first_dst[:, js], low[:, js, 0]))
                for j in range(j0, j1):
                    ins = v.tensor_scalar(moves[:, j, :], low[:, j, :], first_dst[:, j:j + 1], 0.0, ALU.subtract, ALU.max)
                link(ins)
                link(v.scalar_tensor_tensor(window[1][:, js, :], window[0][:, js, :], HIGH_BITS, moves[:, js, :],
                                            ALU.bitwise_and, ALU.bitwise_or))
                for bit in range(SHIFT_BITS):
                    step = 1 << bit
                    old, new = 1 - bit % 2, bit % 2
                    put = min(WINDOW, P + (1 << SHIFT_BITS) - 2 * step)
                    read = min(WINDOW, put + step)
                    link(v.tensor_scalar(moves[:, js, 0:read], window[old][:, js, 0:read], 31 - bit, 31,
                                         ALU.logical_shift_left, ALU.arith_shift_right))
                    link(v.scalar_tensor_tensor(window[new][:, js, 0:put], moves[:, js, 0:put], -1, window[old][:, js, 0:put],
                                                ALU.bitwise_xor, ALU.bitwise_and))
                    link(v.copy_predicated(window[new][:, js, 0:read - step], moves[:, js, step:read], window[old][:, js, step:read]))
                final = window[1 - SHIFT_BITS % 2]
                v.tensor_scalar(pair_field[:, 0, js, :], final[:, js, 0:P], 16, None, ALU.logical_shift_right)
                link(v.tensor_scalar(pair_field[:, 1, js, :], final[:, js, 0:P], 0xFFFF, None, ALU.bitwise_and))
                for j in range(j0, j1):
                    v.tensor_scalar(pair_value[:, 1, j, :], pair_field[:, 1, j, :], first_dst[:, j:j + 1], None, ALU.add)
                v.tensor_copy(pair_value[:, 0, js, :], pair_field[:, 0, js, :]).then_inc(fields_done, 1)

            pack(0, 1)
            dve.wait_ge(fields_turned, 1)
            v.tensor_copy(chunk_src[:, 0:SPREAD], bank[0][:, 0:SPREAD]).then_inc(chunks_known, 1)
            v.tensor_copy(chunk_dst[:, 0:SPREAD], bank[0][:, SPREAD:2 * SPREAD]).then_inc(chunks_known, 1)
            dve.wait_ge(table_landed, 48)
            link(v.tensor_tensor(thirds[:, 0:TILES], bounds_row[:, 1:TILES + 1, 0], bounds_row[:, 0:TILES, 1], ALU.is_gt))
            link(v.reduce_sum(trio_thirds[:], thirds[:].rearrange("a (t q) -> a t q", q=TRIO), AXIS_X))
            v.tensor_copy(table_row[:, :, TRIO_TABLE - 1], trio_thirds[:]).then_inc(thirds_done, 1)
            pack(1, COLUMNS)
            dve.wait_ge(fields_turned, 2)
            v.tensor_copy(chunk_src[:, SPREAD:ENTRIES], bank[0][:, 0:ENTRIES - SPREAD]).then_inc(chunks_known, 1)
            v.tensor_copy(chunk_dst[:, SPREAD:ENTRIES], bank[1][:, 0:ENTRIES - SPREAD]).then_inc(chunks_known, 1)
            dve.wait_ge(chunks_known, 4)

            def check():
                link(v.tensor_tensor(flag_a[:], edge_dst[:, 1:EDGE_COLS + 1], edge_dst[:, 0:EDGE_COLS], ALU.is_lt))
                v.reduce_sum(checks[0:EDGE_ROWS, 0:1], flag_a[:], AXIS_X)
                link(v.tensor_tensor(drift_out[:], drift[:], drift_in[:], ALU.not_equal))
                v.reduce_sum(checks[0:SPREAD, 2:3], drift_out[:], AXIS_X)
                link(v.scalar_tensor_tensor(cover[:], bounds_row[:, 0:TILES, 1], float(P * (SPAN - 2)), bounds_row[:, 1:TILES + 1, 0],
                                            ALU.add, ALU.is_lt))
                v.reduce_sum(check_all[:, 1:2], cover[:], AXIS_X)
                link(v.tensor_tensor(length[:], bounds_row[:, 1:CHUNKS + 1, 2], bounds_row[:, 0:CHUNKS, 2], ALU.subtract))
                link(v.tensor_scalar(too_long[:], length[:], float(WINDOW), None, ALU.is_gt))
                link(v.reduce_sum(check_all[:, 2:3], too_long[:], AXIS_X))
                v.tensor_copy(checks[0:1, 1:2], check_all[:, 1:2])
                v.tensor_copy(checks[0:1, 3:4], check_all[:, 2:3]).then_inc(checks_done, 1)

            def conclude():
                dve.wait_ge(checks_summed, 1)
                link(v.tensor_copy(check_sums[:], sum_bank[0][0:1, 0:6]))
                link(v.tensor_scalar(check_sums[:, 4:5], check_sums[:, 4:5], float(PACKED), None, ALU.not_equal))
                link(v.reduce_sum(check_all[:, 0:1], check_sums[:], AXIS_X))
                link(v.tensor_scalar(k.needs_general[:], check_all[:, 0:1], 0.0, None, ALU.is_gt))

            def load_words(t, u):
                return load_table(dve, t + u, tiles_of(t + u)[0])

            def pick_chunks(t, u, words, tiles, s0, s1):
                for q in tiles:
                    n = (t + u) * TRIO + q
                    first_chunk = dve.snap(words[q][SPAN], min_val=0, max_val=CHUNKS - 1)
                    ins = v.scalar_tensor_tensor(pick[u % 2][:, q, s0:s1, :], column3[:, s0:s1, :], tile_base[:, bass.ds(n, 1)],
                                                 chunk_dst[:, bass.ds(first_chunk + s0, s1 - s0)].unsqueeze(2).to_broadcast([P, s1 - s0, P]),
                                                 ALU.add, ALU.is_equal)
                return ins

            def first_picks(t, u, words):
                tau = t + u
                if not (isinstance(tau, int) and tau < 2):
                    dve.wait_ge(tiles_summed, (tau - 1) * TRIO)
                if tiles_of(tau)[0] > 1:
                    pick_chunks(t, u, words, range(tiles_of(tau)[0] - 1), 0, SPAN - 1)

            def last_picks(t, u, words):
                tiles = tiles_of(t + u)[0]
                with dve.If(dve.snap(words[TRIO][0], min_val=0, max_val=TRIO) > 0):
                    pick_chunks(t, u, words, range(tiles), SPAN - 1, SPAN)
                pick_chunks(t, u, words, range(tiles - 1, tiles), 0, SPAN - 1).then_inc(pick_built, 1)
                free_table(dve, words)

            def add_degrees(t, u):
                tau, b = t + u, u % 2
                tiles, rows = tiles_of(tau)
                dve.wait_ge(h_done, tau + 1)
                for q in range(tiles):
                    ins = v.scalar_tensor_tensor(with_degree[b][0:rows, q, :], k.bn[0:rows, :], sums[u % DEEP][0:rows, q, DIM:DIM + 1],
                                                 h_bank[b][0:rows, q * DIM:q * DIM + DIM], ALU.mult, ALU.add)
                ins.then_inc(h_used, 1)

            def residual(t, u):
                tau, b = t + u, u % 2
                tiles, rows = tiles_of(tau)
                dve.wait_ge(h_used, tau + 1)
                if not (isinstance(tau, int) and tau < DEEP):
                    dve.wait_ge(result_done, tau - (DEEP - 1))
                v.scalar_tensor_tensor(y[u % DEEP][0:rows, 0:tiles, :], with_degree[b][0:rows, 0:tiles, :], 0.0,
                                       x_in[u % DEEP][0:rows, 0:tiles, :], ALU.max, ALU.add).then_inc(y_done, 1)

            def statistics(t, u):
                tau, b = t + u, u % DEEP
                tiles, rows = tiles_of(tau)
                dve.wait_ge(y_done, tau + 1)
                for q in range(tiles):
                    ins = v.bn_stats(stats[b][0:rows, q, :], y[b][0:rows, q, :])
                ins.then_inc(stats_done, 1)

            def aggregate(t, u):
                tau, b = t + u, u % DEEP
                tiles, rows = tiles_of(tau)
                for q in range(tiles):
                    ins = v.bn_aggr(mean_var[b][0:rows, q, :], stats[b][0:rows, q, :])
                ins.then_inc(mean_var_done, 1)

            def scales(t, u):
                tau, b = t + u, u % DEEP
                tiles, rows = tiles_of(tau)
                dve.wait_ge(std_done, tau + 1)
                v.reciprocal(rstd[b][0:rows, 0:tiles], std[b][0:rows, 0:tiles]).then_inc(rstd_done, 1)
                if not (isinstance(tau, int) and tau + 1 >= TRIOS):
                    dve.wait_ge(stats_done, tau + 2)
                dve.wait_ge(rstd_done, tau + 1)
                v.scalar_tensor_tensor(minus_mean[b][0:rows, 0:tiles], mean_var[b][0:rows, 0:tiles, 0], -1.0,
                                       rstd[b][0:rows, 0:tiles], ALU.mult, ALU.mult).then_inc(norm_ready, 1)

            def step(t, u):
                tau = t + u
                known = isinstance(tau, int)
                picks = not known or tau + 2 < TRIOS
                rest = not known or 1 <= tau <= TRIOS
                if rest:
                    add_degrees(t, u - 1)
                if picks:
                    words = load_words(t, u + 2)
                    first_picks(t, u + 2, words)
                if rest:
                    residual(t, u - 1)
                if picks:
                    last_picks(t, u + 2, words)
                if rest:
                    statistics(t, u - 1)
                if known and tau == 1:
                    dve.wait_ge(stats_done, 1)
                if (not known or tau >= 2) and (not known or tau - 2 < TRIOS):
                    scales(t, u - 2)
                if rest:
                    aggregate(t, u - 1)

            dve.wait_ge(k.bn_landed, 16)
            for u in range(2):
                words = load_words(0, u)
                first_picks(0, u, words)
                last_picks(0, u, words)
            for u in range(DEEP):
                step(0, u)
            check()
            with dve.Fori(DEEP, LOOPED - DEEP + 1, DEEP) as t:
                for u in range(DEEP):
                    step(t, u)
            for u in range(TRIOS + 2 - LOOPED):
                step(LOOPED, u)
            conclude()

        @block_.tensor
        def _(pe):
            mm = nc.tensor.matmul
            pe.wait_ge(k.consts_made, 1)
            pe.wait_ge(row_counts, 1)
            mm(bank[0][0:EDGE_ROWS, 0:1], k.before[0:EDGE_ROWS, 0:EDGE_ROWS], kept_upto[:, EDGE_COLS - 1:EDGE_COLS],
               start=True, stop=True).then_inc(rows_summed, 1)
            pe.wait_ge(k.consts_made, 2)
            for i, w in enumerate((k.ws, k.wn, k.wsum)):
                nc.tensor.transpose(bank[2 + i][:, 0:P], w[:], k.identity[:]).then_inc(k.weights_turned, 1)
            pe.wait_ge(fields_done, 1)
            nc.tensor.transpose(bank[0][:, 0:SPREAD], pair_value[:, 0, 0, :], k.identity[0:SPREAD, 0:SPREAD])
            nc.tensor.transpose(bank[0][:, SPREAD:2 * SPREAD], pair_value[:, 1, 0, :],
                                k.identity[0:SPREAD, 0:SPREAD]).then_inc(fields_turned, 1)
            pe.wait_ge(fields_done, 2)
            for a in range(2):
                for j in range(1, COLUMNS):
                    ins = nc.tensor.transpose(bank[a][:, (j - 1) * SPREAD:j * SPREAD], pair_value[:, a, j, :],
                                              k.identity[0:SPREAD, 0:SPREAD])
            ins.then_inc(fields_turned, 1)

            def turn_x(t, u):
                tau, b = t + u, u % 2
                tiles, rows = tiles_of(tau)
                pe.wait_ge(x_landed[u % DEEP], 4 * (t + u // DEEP * DEEP) + 16)
                if not (isinstance(tau, int) and tau < 2):
                    pe.wait_ge(xt_copied, tau - 1)
                for q in range(tiles):
                    ins = nc.tensor.transpose(xt_bank[b][:, q * P:q * P + rows], x_in[u % DEEP][0:rows, q, :], k.identity[0:rows, 0:rows])
                ins.then_inc(xt_turned, 1)

            def sum_rows(t, u):
                tau, b = t + u, u % 2
                known = isinstance(tau, int)
                pe.wait_ge(pick_built, tau + 1)
                if not known or tau >= 2:
                    pe.wait_ge(sums_copied, tau - 1)
                tiles, _ = tiles_of(tau)
                words = load_table(pe, tau, tiles)

                def chunk_product(q, s):
                    slot = pe.snap(words[q][s], min_val=0, max_val=(RING - 1) * ROW)
                    return mm(sum_bank[b][:, q * ROW:q * ROW + DIM + 1], pick[b][:, q, s, :],
                              ring[:].rearrange("p c w -> p (c w)")[:, bass.ds(slot, DIM + 1)],
                              start=(q == 0 and s == 0), stop=(q == tiles - 1 and s == 1))

                for q in range(tiles):
                    ahead = u * TRIO + q + DRIFT + SPAN - 1
                    n = tau * TRIO + q
                    if known and tau == 0 and q == 0:
                        for c in range(ahead):
                            pe.wait_ge(gathered[c % GATHER_SEMS], 16)
                    if not known or n + DRIFT + SPAN - 1 < CHUNKS:
                        pe.wait_ge(gathered[ahead % GATHER_SEMS], 4 * t + 16 * (ahead // GATHER_SEMS + 1))
                    chunk_product(q, 0)
                with pe.If(pe.snap(words[TRIO][0], min_val=0, max_val=TRIO) > 0):
                    for q in range(tiles):
                        chunk_product(q, 2)
                for q in range(tiles):
                    chunk_product(q, 1).then_inc(tiles_summed, 1)
                free_table(pe, words)

            def turn_sums(t, u):
                tau, b = t + u, u % 2
                pe.wait_ge(sums_copied, tau + 1)
                if not (isinstance(tau, int) and tau < 2):
                    pe.wait_ge(st_copied, tau - 1)
                for q in range(tiles_of(tau)[0]):
                    ins = nc.tensor.transpose(st_bank[b][:, q * P:q * P + P], sums[u % DEEP][:, q, 0:DIM], k.identity[:])
                ins.then_inc(st_turned, 1)

            def products(t, u):
                tau, b = t + u, u % 2
                tiles, rows = tiles_of(tau)
                pe.wait_ge(st_copied, tau + 1)
                pe.wait_ge(xt_copied, tau + 1)
                if not (isinstance(tau, int) and tau < 2):
                    pe.wait_ge(h_used, tau - 1)
                for q in range(tiles):
                    h = h_bank[b][0:rows, q * DIM:q * DIM + DIM]
                    mm(h, k.ones_bf[0:3, 0:rows], k.bsn3[:], start=True, stop=False)
                    mm(h, x_t[b][:, q, 0:rows], k.wsum_t[:], start=False, stop=False)
                    ins = mm(h, sums_t[b][:, q, 0:rows], k.wn_t[:], start=False, stop=True)
                ins.then_inc(h_done, 1)

            def step(t, u):
                tau = t + u
                known = isinstance(tau, int)
                turn_sums(t, u)
                if not known or tau + 1 < TRIOS:
                    sum_rows(t, u + 1)
                    turn_x(t, u + 1)
                products(t, u)

            pe.wait_ge(k.weights_copied, 3)
            pe.wait_ge(k.parts_landed, 16)
            pe.wait_ge(table_landed, 48)
            pe.wait_ge(thirds_done, 1)
            pe.wait_ge(ones_set, 1)
            turn_x(0, 0)
            sum_rows(0, 0)
            for u in range(DEEP):
                step(0, u)
            with pe.Fori(DEEP, LOOPED - DEEP + 1, DEEP) as t:
                for u in range(DEEP):
                    step(t, u)
            for u in range(TRIOS - LOOPED):
                step(LOOPED, u)
            pe.wait_ge(checks_done, 1)
            pe.wait_ge(sums_copied, TRIOS)
            mm(sum_bank[0][0:1, 0:6], k.ones[:, 0:1], checks[:], start=True, stop=True).then_inc(checks_summed, 1)

        @block_.scalar
        def _(act):
            for i, w_t in enumerate((k.ws_t, k.wn_t, k.wsum_t)):
                act.wait_ge(k.weights_turned, i + 1)
                nc.scalar.copy(w_t[:], bank[2 + i][:, 0:P]).then_inc(k.weights_copied, 1)

            def copy_sums(t, u):
                tau, b = t + u, u % 2
                tiles, _ = tiles_of(tau)
                act.wait_ge(tiles_summed, tau * TRIO + tiles)
                nc.scalar.copy(sums[u % DEEP][:, 0:tiles, 0:DIM + 1],
                               sum_bank[b][:, 0:TRIO * ROW].rearrange("p (q w) -> p q w", q=TRIO)[:, 0:tiles, 0:DIM + 1]
                               ).then_inc(sums_copied, 1)

            def copy_sums_t(t, u):
                tau, b = t + u, u % 2
                tiles, _ = tiles_of(tau)
                act.wait_ge(st_turned, tau + 1)
                nc.scalar.copy(sums_t[b][:, 0:tiles, :], st_bank[b][:, 0:tiles * P].rearrange("p (q w) -> p q w", q=tiles)
                               ).then_inc(st_copied, 1)

            def copy_x_t(t, u):
                tau, b = t + u, u % 2
                tiles, rows = tiles_of(tau)
                act.wait_ge(xt_turned, tau + 1)
                nc.scalar.copy(x_t[b][:, 0:tiles, 0:rows],
                               xt_bank[b][:, 0:tiles * P].rearrange("p (q w) -> p q w", q=tiles)[:, :, 0:rows]
                               ).then_inc(xt_copied, 1)

            def deviation(t, u):
                tau, b = t + u, u % DEEP
                tiles, rows = tiles_of(tau)
                act.wait_ge(mean_var_done, tau + 1)
                nc.scalar.activation(std[b][0:rows, 0:tiles], mean_var[b][0:rows, 0:tiles, 1], ACT.Sqrt,
                                     bias=k.eps[0:rows, 0:1], scale=1.0).then_inc(std_done, 1)

            def normalise(t, u):
                tau, b = t + u, u % DEEP
                tiles, rows = tiles_of(tau)
                act.wait_ge(norm_ready, tau + 1)
                if not (isinstance(tau, int) and tau < DEEP):
                    act.wait_ge(stored[b], 4 * (t + u // DEEP * DEEP))
                for q in range(tiles):
                    ins = nc.scalar.activation(result[b][0:rows, q, :], y[b][0:rows, q, :], ACT.Identity,
                                               bias=minus_mean[b][0:rows, q:q + 1], scale=rstd[b][0:rows, q:q + 1])
                ins.then_inc(result_done, 1)

            def step(t, u):
                tau = t + u
                known = isinstance(tau, int)
                if not known or tau < TRIOS:
                    copy_sums_t(t, u)
                if not known or 2 <= tau < TRIOS + 2:
                    deviation(t, u - 2)
                if not known or tau >= 3:
                    normalise(t, u - 3)
                if not known or tau + 1 < TRIOS:
                    copy_sums(t, u + 1)
                    copy_x_t(t, u + 1)

            copy_x_t(0, 0)
            copy_sums(0, 0)
            for u in range(DEEP):
                step(0, u)
            with act.Fori(DEEP, LOOPED - DEEP + 1, DEEP) as t:
                for u in range(DEEP):
                    step(t, u)
            for u in range(TRIOS + 3 - LOOPED):
                step(LOOPED, u)


def build_general_case(nc, ctx, k, x, src, dst, out):
    def sb(name, shape, dtype=FP32):
        return ctx.enter_context(nc.sbuf_tensor(name, shape, dtype))

    def sem(name):
        return ctx.enter_context(nc.semaphore(name))

    sums_dram = nc.dram_tensor("sums_dram", (SUM_ROWS, ROW), FP32, kind="Internal").ap()
    zero_rows = sb("zero_rows", [P, ZERO_ROWS * ROW])
    bs = sb("bs", [P, DIM])
    dst_line = sb("dst_line", [GEN_EDGES, GEN_EDGES], INT32)
    dst_own = sb("dst_own", [GEN_EDGES, 1], INT32)
    src_own = sb("src_own", [GEN_EDGES, 1], INT32)
    dst_value = sb("dst_value", [GEN_EDGES, 1])
    spare_row = sb("spare_row", [GEN_EDGES, 1])
    earlier = sb("earlier", [GEN_EDGES, GEN_EDGES])
    same = sb("same", [GEN_EDGES, GEN_EDGES])
    same_earlier = sb("same_earlier", [GEN_EDGES, GEN_EDGES])
    repeats = sb("repeats", [GEN_EDGES, 1])
    is_repeat = sb("is_repeat", [GEN_EDGES, 1])
    to_spare = sb("to_spare", [GEN_EDGES, 1])
    moved = sb("moved", [GEN_EDGES, 1])
    target = sb("target", [GEN_EDGES, 1], INT32)
    rows = sb("rows", [GEN_EDGES, ROW])
    totals = sb("totals", [GEN_EDGES, ROW])
    x_rows = sb("x_rows", [GEN_ROWS, DIM])
    sum_rows = sb("sum_rows", [GEN_ROWS, ROW])
    x_turned = sb("x_turned", [P, 2, GEN_ROWS])
    biased = sb("biased", [GEN_ROWS, DIM])
    before_relu = sb("before_relu", [GEN_ROWS, DIM])
    y = sb("gen_y", [GEN_ROWS, DIM])
    stats = sb("gen_stats", [GEN_ROWS, 6])
    mean_var = sb("gen_mean_var", [GEN_ROWS, 2])
    std = sb("gen_std", [GEN_ROWS, 1])
    rstd = sb("gen_rstd", [GEN_ROWS, 1])
    result = sb("gen_result", [GEN_ROWS, DIM])
    totals_bank = ctx.enter_context(nc.psum_tensor("totals_bank", [P, 512], FP32))
    turn_bank = ctx.enter_context(nc.psum_tensor("turn_bank", [P, 512], FP32))
    h_bank = ctx.enter_context(nc.psum_tensor("gen_h_bank", [P, 512], FP32))

    zeros_set = sem("gen_zeros_set")
    zeroed = sem("gen_zeroed")
    bs_landed = sem("gen_bs_landed")
    step_landed = sem("gen_step_landed")
    rows_wanted = sem("gen_rows_wanted")
    rows_landed = sem("gen_rows_landed")
    same_done = sem("gen_same_done")
    target_done = sem("gen_target_done")
    totals_done = sem("gen_totals_done")
    totals_copied = sem("gen_totals_copied")
    adds_wanted = sem("gen_adds_wanted")
    added = sem("gen_added")
    order = sem("gen_order")
    tile_landed = sem("gen_tile_landed")
    turned = sem("gen_turned")
    turned_copied = sem("gen_turned_copied")
    h_done = sem("gen_h_done")
    var_done = sem("gen_var_done")
    std_done = sem("gen_std_done")
    result_done = sem("gen_result_done")
    stored = sem("gen_stored")

    EDGE_LINKS = 9
    TILE_LINKS = 5

    def only_if_needed(engine, program):
        needed = engine.value_load(k.needs_general[0:1, 0:1], min_val=0, max_val=1)
        with engine.If(needed > 0):
            program(engine)
            engine.nop()
        with engine.Else():
            engine.nop()
        engine.nop()

    with nc.Block() as block:
        @block.sync
        def _(sp):
            def program(sp):
                sp.dma_start(bs[:], k.inputs[1].rearrange("(a d) -> a d", a=1).partition_broadcast(P)).then_inc(bs_landed, 16)
                sp.wait_ge(zeros_set, 1)
                zero_view = sums_dram.rearrange("(z p r) w -> z p (r w)", p=P, r=ZERO_ROWS)
                for z in range(SUM_ROWS // (P * ZERO_ROWS)):
                    sp.dma_start(zero_view[z, :, :], zero_rows[:]).then_inc(zeroed, 16)
                sp.sem_inc(added, 16)
                with sp.Fori(0, GEN_STEPS, 1) as s:
                    edges = bass.ds(s * GEN_EDGES, GEN_EDGES)
                    sp.wait_ge(added, s * 16 + 16)
                    sp.dma_start(dst_line[:], dst[edges].rearrange("(a e) -> a e", a=1).partition_broadcast(GEN_EDGES)).then_inc(step_landed, 16)
                    sp.dma_start(dst_own[:], dst[edges].rearrange("(e a) -> e a", a=1)).then_inc(step_landed, 16)
                    sp.dma_start(src_own[:], src[edges].rearrange("(e a) -> e a", a=1)).then_inc(step_landed, 16)
                sp.wait_ge(added, GEN_STEPS * 16 + 16)
                sp.sem_inc(result_done, 1)
                with sp.Fori(0, GEN_TILES, 1) as n:
                    nodes = bass.ds(n * GEN_ROWS, GEN_ROWS)
                    sp.wait_ge(result_done, n + 1)
                    sp.dma_start(x_rows[:], x[nodes, :]).then_inc(tile_landed, 16)
                    sp.dma_start(sum_rows[:], sums_dram[nodes, :]).then_inc(tile_landed, 16)

            only_if_needed(sp, program)

        @block.gpsimd
        def _(pool):
            def program(pool):
                pool.wait_ge(zeroed, 16 * (SUM_ROWS // (P * ZERO_ROWS)))
                with pool.Fori(0, GEN_STEPS, 1) as s:
                    pool.wait_ge(step_landed, s * 48 + 48)
                    pool.sem_inc(rows_wanted, 1)
                    nc.gpsimd.indirect_dma_start(rows[:, 0:DIM], None, x,
                                                 bass.IndirectOffsetOnAxis(ap=src_own[:, 0:1], axis=0)).then_inc(rows_landed, 16)
                    pool.wait_ge(target_done, s + 1)
                    pool.wait_ge(totals_copied, s + 1)
                    pool.sem_inc(adds_wanted, 1)
                    nc.gpsimd.indirect_dma_start(sums_dram, bass.IndirectOffsetOnAxis(ap=target[:, 0:1], axis=0), totals[:], None,
                                                 compute_op=ALU.add).then_inc(added, 16)

            only_if_needed(pool, program)

        @block.vector
        def _(dve):
            def program(dve):
                v = nc.vector
                v.memset(zero_rows[:], 0.0).then_inc(zeros_set, 1)
                v.memset(rows[:, DIM:DIM + 1], 1.0)
                v.memset(rows[:, DIM + 1:ROW], 0.0)
                v.tensor_scalar(spare_row[:], k.partition[0:GEN_EDGES, :], float(NODES), None, ALU.add)
                v.tensor_scalar(earlier[:], k.column[0:GEN_EDGES, 0:GEN_EDGES], k.partition[0:GEN_EDGES, 0:1], None, ALU.is_lt).then_inc(zeros_set, 1)
                dve.wait_ge(zeros_set, 2)
                with dve.Fori(0, GEN_STEPS, 1) as s:
                    links = [0]

                    def link(ins):
                        links[0] += 1
                        ins.then_inc(order, 1)
                        dve.wait_ge(order, s * EDGE_LINKS + links[0])

                    dve.wait_ge(step_landed, s * 48 + 48)
                    link(v.tensor_copy(dst_value[:], dst_own[:]))
                    v.tensor_scalar(same[:], dst_line[:], dst_value[:, 0:1], None, ALU.is_equal).then_inc(same_done, 1)
                    dve.wait_ge(same_done, s + 1)
                    link(v.tensor_tensor(same_earlier[:], same[:], earlier[:], ALU.mult))
                    link(v.reduce_sum(repeats[:], same_earlier[:], AXIS_X))
                    link(v.tensor_scalar(is_repeat[:], repeats[:], 0.0, None, ALU.is_gt))
                    link(v.tensor_tensor(to_spare[:], spare_row[:], dst_value[:], ALU.subtract))
                    link(v.tensor_tensor(moved[:], to_spare[:], is_repeat[:], ALU.mult))
                    link(v.tensor_tensor(moved[:], moved[:], dst_value[:], ALU.add))
                    v.tensor_copy(target[:], moved[:]).then_inc(target_done, 1)
                    dve.wait_ge(target_done, s + 1)
                    dve.wait_ge(totals_done, s + 1)
                    link(v.tensor_copy(totals[:, 0:DIM], totals_bank[0:GEN_EDGES, 0:DIM]))
                    link(v.tensor_copy(totals[:, DIM:ROW], totals_bank[0:GEN_EDGES, DIM:ROW]))
                    dve.sem_inc(totals_copied, 1)
                dve.wait_ge(bs_landed, 16)
                dve.sem_inc(stored, 16)
                with dve.Fori(0, GEN_TILES, 1) as n:
                    links = [0]

                    def link(ins):
                        links[0] += 1
                        ins.then_inc(order, 1)
                        dve.wait_ge(order, n * TILE_LINKS + (GEN_STEPS * EDGE_LINKS + links[0]))

                    dve.wait_ge(h_done, n + 1)
                    link(v.tensor_tensor(biased[:], bs[0:GEN_ROWS, :], h_bank[0:GEN_ROWS, 0:DIM], ALU.add))
                    link(v.scalar_tensor_tensor(before_relu[:], k.bn[0:GEN_ROWS, :], sum_rows[:, DIM:DIM + 1], biased[:], ALU.mult, ALU.add))
                    link(v.scalar_tensor_tensor(y[:], before_relu[:], 0.0, x_rows[:], ALU.max, ALU.add))
                    link(v.bn_stats(stats[:], y[:]))
                    dve.sem_inc(zeros_set, 1)
                    v.bn_aggr(mean_var[:], stats[:]).then_inc(var_done, 1)
                    dve.wait_ge(std_done, n + 1)
                    link(v.reciprocal(rstd[:], std[:]))
                    dve.wait_ge(stored, n * 16 + 16)
                    v.tensor_scalar(result[:], y[:], mean_var[:, 0:1], rstd[:, 0:1], ALU.subtract, ALU.mult).then_inc(result_done, 1)

            only_if_needed(dve, program)

        @block.tensor
        def _(pe):
            def program(pe):
                mm = nc.tensor.matmul
                pe.wait_ge(zeros_set, 2)
                with pe.Fori(0, GEN_STEPS, 1) as s:
                    pe.wait_ge(same_done, s + 1)
                    pe.wait_ge(rows_landed, s * 16 + 16)
                    mm(totals_bank[0:GEN_EDGES, 0:ROW], same[:], rows[:], start=True, stop=True).then_inc(totals_done, 1)
                with pe.Fori(0, GEN_TILES, 1) as n:
                    pe.wait_ge(tile_landed, n * 32 + 32)
                    nc.tensor.transpose(turn_bank[:, 0:GEN_ROWS], x_rows[:], k.identity[0:GEN_ROWS, 0:GEN_ROWS])
                    nc.tensor.transpose(turn_bank[:, GEN_ROWS:2 * GEN_ROWS], sum_rows[:, 0:DIM],
                                        k.identity[0:GEN_ROWS, 0:GEN_ROWS]).then_inc(turned, 1)
                    pe.wait_ge(turned_copied, n + 1)
                    mm(h_bank[0:GEN_ROWS, 0:DIM], x_turned[:, 0, :], k.ws_t[:], start=True, stop=False)
                    mm(h_bank[0:GEN_ROWS, 0:DIM], x_turned[:, 1, :], k.wn_t[:], start=False, stop=True).then_inc(h_done, 1)

            only_if_needed(pe, program)

        @block.scalar
        def _(act):
            def program(act):
                with act.Fori(0, GEN_TILES, 1) as n:
                    act.wait_ge(turned, n + 1)
                    nc.scalar.copy(x_turned[:], turn_bank[:, 0:2 * GEN_ROWS].rearrange("p (a r) -> p a r", a=2)).then_inc(turned_copied, 1)
                    act.wait_ge(var_done, n + 1)
                    nc.scalar.activation(std[:], mean_var[:, 1:2], ACT.Sqrt, bias=k.eps[0:GEN_ROWS, 0:1], scale=1.0).then_inc(std_done, 1)
                    act.wait_ge(result_done, n + 2)
                    act.dma_start(out[bass.ds(n * GEN_ROWS, GEN_ROWS), :], result[:]).then_inc(stored, 16)
                act.wait_ge(stored, GEN_TILES * 16 + 16)

            only_if_needed(act, program)


INPUTS = ["x", "src", "dst", "L0_gnn_W_self", "L0_gnn_b_self", "L0_gnn_W_neigh", "L0_gnn_b_neigh"]


def kernel(**inputs):
    import concourse.bacc as bacc
    from concourse.bass_utils import run_bass_kernel_spmd

    nc = bacc.Bacc("TRN2", target_bir_lowering=False, num_devices=1)
    arrays, args = {}, []
    for name in INPUTS:
        a = np.ascontiguousarray(inputs[name])
        arrays[f"in_{name}"] = a
        args.append(nc.dram_tensor(f"in_{name}", a.shape, mybir.dt.from_np(a.dtype), kind="ExternalInput").ap())
    out = nc.dram_tensor("out", (NODES, DIM), FP32, kind="ExternalOutput").ap()
    gnn_kernel(nc, *args, out)
    done = run_bass_kernel_spmd(nc, [arrays], core_ids=[0])
    return done.results[0]["out"]
```

```python
import numpy as np

import concourse.bass as bass
from concourse import mybir
from contextlib import ExitStack

FP32 = mybir.dt.float32
BF16 = mybir.dt.bfloat16
INT32 = mybir.dt.int32
ALU = mybir.AluOpType
ACT = mybir.ActivationFunctionType
AXIS_X = mybir.AxisListType.X

P = 128
NODES, DIM, EDGES = 50000, 128, 100000
EPS = 1e-5

EDGE_ROWS = 125
EDGE_COLS = EDGES // EDGE_ROWS
BLOCK = 200
BLOCKS = EDGES // BLOCK
BLOCKS_PER_ROW = EDGE_COLS // BLOCK

TILES = -(-NODES // P)
LAST_ROWS = NODES - (TILES - 1) * P
PACKED = EDGES - NODES
CHUNKS = -(-PACKED // P)
COLUMNS = 4
SPREAD = -(-(CHUNKS + 1) // COLUMNS)
ENTRIES = SPREAD * COLUMNS

WINDOW = 312
SHIFT_BITS = 8
HIGH_BITS = -(1 << 16)
PAD = 400
NO_NODE = 65535

SPAN = 3
DRIFT = 8
RING = 96
STAGE = 16
GATHER_SEMS = 12
ROW = DIM + 4
TABLE = SPAN + 1

TRIO = 3
TRIOS = -(-TILES // TRIO)
TRIO_TABLE = TRIO * TABLE + 1
DEEP = 4

UNROLL = 2 * DEEP
START = 2 * DEEP
PARTS = 3
BIAS_ROWS = (TRIO + 1) * PARTS
MAX_DEGREE = 256
LOOPED = START + ((CHUNKS - DRIFT - SPAN) // TRIO - 1 - START) // UNROLL * UNROLL

GEN_EDGES = 125
GEN_STEPS = EDGES // GEN_EDGES
GEN_ROWS = 125
GEN_TILES = NODES // GEN_ROWS
ZERO_ROWS = 28
SUM_ROWS = 14 * P * ZERO_ROWS


def gnn_kernel(nc, x, src, dst, w_self, b_self, w_neigh, b_neigh, out):
    with ExitStack() as ctx:
        def sb(name, shape, dtype=FP32):
            return ctx.enter_context(nc.sbuf_tensor(name, shape, dtype))

        def sem(name):
            return ctx.enter_context(nc.semaphore(name))

        weights = build_constants(nc, sb, sem, w_self, b_self, w_neigh, b_neigh)
        with ExitStack() as fast:
            build_common_case(nc, fast, weights, x, src, dst, out)
        with ExitStack() as general:
            build_general_case(nc, general, weights, x, src, dst, out)


class Constants:
    pass


def build_constants(nc, sb, sem, w_self, b_self, w_neigh, b_neigh):
    k = Constants()
    k.column = sb("column", [P, P])
    k.partition = sb("partition", [P, 1])
    k.identity = sb("identity", [P, P])
    k.before = sb("before", [P, P])
    k.ones = sb("ones", [P, 1])
    k.eps = sb("eps", [P, 1])
    k.ws = sb("ws", [P, DIM])
    k.wn = sb("wn", [P, DIM])
    k.wsum = sb("wsum", [P, DIM])
    k.ws_t = sb("ws_t", [P, DIM])
    k.wn_t = sb("wn_t", [P, DIM])
    k.wsum_t = sb("wsum_t", [P, DIM])
    k.bn = sb("bn", [P, DIM])
    k.bs_row = sb("bs_row", [1, DIM])
    k.bn_row = sb("bn_row", [1, DIM])
    k.bias_row = sb("bias_row", [1, 2, DIM])
    k.bias_rest = sb("bias_rest", [1, 2, 2, DIM])
    k.bias_part = sb("bias_part", [1, 3, 2, DIM], BF16)
    k.bias = sb("bias", [BIAS_ROWS, TRIO, DIM], BF16)
    k.needs_general = sb("needs_general", [1, 1], INT32)
    return_sems(k, sem)
    k.inputs = (w_self, b_self, w_neigh, b_neigh)
    return k


def return_sems(k, sem):
    k.iotas = sem("iotas")
    k.weights_landed = sem("weights_landed")
    k.bn_landed = sem("bn_landed")
    k.consts_made = sem("consts_made")
    k.weights_turned = sem("weights_turned")
    k.weights_copied = sem("weights_copied")
    k.parts_made = sem("parts_made")
    k.parts_landed = sem("parts_landed")


def build_common_case(nc, ctx, k, x, src, dst, out):
    def sb(name, shape, dtype=FP32):
        return ctx.enter_context(nc.sbuf_tensor(name, shape, dtype))

    def sem(name):
        return ctx.enter_context(nc.semaphore(name))

    def scratch(name, shape, dtype):
        return nc.dram_tensor(name, shape, dtype, kind="Internal").ap()

    w_self, b_self, w_neigh, b_neigh = k.inputs

    words_padded = scratch("words_padded", (EDGES + PAD, 1), INT32)
    kept_upto_dram = scratch("kept_upto_dram", (BLOCKS, BLOCK), FP32)
    ends_dram = scratch("ends_dram", (1, EDGE_ROWS * 2 * BLOCKS_PER_ROW), FP32)
    table_dram = scratch("table_dram", (ENTRIES, TABLE), INT32)
    bounds_dram = scratch("bounds_dram", (ENTRIES, 3), FP32)

    edge_src = sb("edge_src", [EDGE_ROWS, EDGE_COLS], INT32)
    edge_dst = sb("edge_dst", [EDGE_ROWS, EDGE_COLS + 1], INT32)
    flag_a = sb("flag_a", [EDGE_ROWS, EDGE_COLS])
    flag_b = sb("flag_b", [EDGE_ROWS, EDGE_COLS])
    zeros = sb("zeros", [EDGE_ROWS, EDGE_COLS])
    kept_upto = sb("kept_upto", [EDGE_ROWS, EDGE_COLS])
    dst_if_kept = sb("dst_if_kept", [EDGE_ROWS, EDGE_COLS], INT32)
    edge_words = sb("edge_words", [EDGE_ROWS, EDGE_COLS], INT32)
    pad_words = sb("pad_words", [1, PAD], INT32)
    rows_before = sb("rows_before", [EDGE_ROWS, 1])
    ends = sb("ends", [EDGE_ROWS, 2, BLOCKS_PER_ROW])
    all_ends = sb("all_ends", [SPREAD, EDGE_ROWS, 2, BLOCKS_PER_ROW])
    below = [sb(f"below{j}", [SPREAD, EDGE_ROWS * BLOCKS_PER_ROW]) for j in range(COLUMNS)]
    length, too_long = (below[i][0:1, 0:CHUNKS] for i in range(2))
    laps = [sb(f"laps{i}", [SPREAD, SPAN, COLUMNS]) for i in range(2)]
    drift_out = sb("drift_out", [SPREAD, COLUMNS])
    limit = sb("limit", [SPREAD, COLUMNS])
    entry = sb("entry", [SPREAD, COLUMNS])
    counts = sb("counts", [SPREAD, 2, COLUMNS])
    block = sb("block", [SPREAD, 2, COLUMNS])
    block_index = sb("block_index", [SPREAD, 2, COLUMNS], INT32)
    in_block = sb("in_block", [SPREAD, 2, COLUMNS])
    kept_block = sb("kept_block", [SPREAD, COLUMNS, BLOCK])
    dst_block = sb("dst_block", [SPREAD, COLUMNS, BLOCK], INT32)
    place = sb("place", [SPREAD, 2, COLUMNS])
    place_index = sb("place_index", [SPREAD, 2, COLUMNS], INT32)
    packed_before = sb("packed_before", [SPREAD, COLUMNS])
    first_int = sb("first_int", [SPREAD, COLUMNS], INT32)
    drift = sb("drift", [SPREAD, COLUMNS])
    drift_in = sb("drift_in", [SPREAD, COLUMNS])
    first = sb("first", [SPREAD, COLUMNS])
    ring_slot = sb("ring_slot", [SPREAD, SPAN, COLUMNS])
    table = sb("table", [SPREAD, COLUMNS, TABLE], INT32)
    table_row = sb("table_row", [1, TRIOS, TRIO_TABLE], INT32)
    bounds = sb("bounds", [SPREAD, COLUMNS, 3])
    bounds_row = sb("bounds_row", [1, ENTRIES, 3])
    cover = sb("cover", [1, TILES])
    thirds = sb("thirds", [1, TRIOS * TRIO])
    trio_thirds = sb("trio_thirds", [1, TRIOS])
    checks = sb("checks", [P, 6])
    check_sums = sb("check_sums", [1, 6])
    check_all = sb("check_all", [1, 3])

    window = [sb(f"window{i}", [SPREAD, COLUMNS, WINDOW], INT32) for i in range(2)]
    low = sb("low", [SPREAD, COLUMNS, WINDOW], INT32)
    moves = sb("moves", [SPREAD, COLUMNS, WINDOW], INT32)
    first_dst = sb("first_dst", [SPREAD, COLUMNS])
    pair_field = sb("pair_field", [SPREAD, 2, COLUMNS, P], INT32)
    pair_value = sb("pair_value", [SPREAD, 2, COLUMNS, P])
    chunk_src = sb("chunk_src", [P, ENTRIES], INT32)
    chunk_dst = sb("chunk_dst", [P, ENTRIES + 1])

    column3 = sb("column3", [P, SPAN, P])
    tile_base = sb("tile_base", [P, TILES])
    staged = sb("staged", [P, RING], INT32)
    ring = sb("ring", [P, RING, ROW])
    x_in = [sb(f"x_in{i}", [P, TRIO, DIM]) for i in range(DEEP)]
    pick = [sb(f"pick{i}", [P, TRIO, SPAN, P]) for i in range(DEEP)]
    sums = [sb(f"sums{i}", [P, TRIO, DIM]) for i in range(DEEP)]
    x_t = [sb(f"x_t{i}", [P, TRIO, P]) for i in range(2)]
    sums_t = [sb(f"sums_t{i}", [P, TRIO, P]) for i in range(2)]
    degrees_n = [sb(f"degrees_n{i}", [P, TRIO * PARTS]) for i in range(DEEP)]
    degrees_t = [sb(f"degrees_t{i}", [BIAS_ROWS, P], BF16) for i in range(2)]
    degrees = sb("degrees", [P, TILES])
    y = [sb(f"y{i}", [P, TRIO, DIM]) for i in range(DEEP)]
    stats = [sb(f"stats{i}", [P, TRIO, 6]) for i in range(DEEP)]
    mean_var = [sb(f"mean_var{i}", [P, TRIO, 2]) for i in range(DEEP)]
    std = [sb(f"std{i}", [P, TRIO]) for i in range(DEEP)]
    rstd = [sb(f"rstd{i}", [P, TRIO]) for i in range(DEEP)]
    minus_mean = [sb(f"minus_mean{i}", [P, TRIO]) for i in range(DEEP)]
    result = [sb(f"result{i}", [P, TRIO, DIM]) for i in range(DEEP)]

    bank = [ctx.enter_context(nc.psum_tensor(f"bank{i}", [P, 512], FP32)) for i in range(8)]
    sum_bank, xt_bank, st_bank, h_bank = bank[0:2], bank[2:4], bank[4:6], bank[6:8]

    edges_landed = sem("edges_landed")
    next_landed = sem("next_landed")
    next_set = sem("next_set")
    pads_set = sem("pads_set")
    padded_stored = sem("padded_stored")
    row_counts = sem("row_counts")
    rows_summed = sem("rows_summed")
    upto_done = sem("upto_done")
    upto_stored = sem("upto_stored")
    ends_done = sem("ends_done")
    ends_stored = sem("ends_stored")
    ends_landed = sem("ends_landed")
    blocks_found = sem("blocks_found")
    block_landed = [sem(f"block_landed{i}") for i in range(2 * COLUMNS)]
    places_found = sem("places_found")
    window_landed = [sem(f"window_landed{i}") for i in range(COLUMNS)]
    table_done = sem("table_done")
    table_stored = sem("table_stored")
    table_landed = sem("table_landed")
    thirds_done = sem("thirds_done")
    words_done = sem("words_done")
    fields_done = sem("fields_done")
    fields_turned = sem("fields_turned")
    chunks_known = sem("chunks_known")
    dve_order = sem("dve_order")
    checks_done = sem("checks_done")
    checks_summed = sem("checks_summed")
    gathered = [sem(f"gathered{i}") for i in range(GATHER_SEMS)]
    stage_done = sem("stage_done")
    slots_free = sem("slots_free")
    ones_set = sem("ones_set")
    x_landed = [sem(f"x_landed{i}") for i in range(DEEP)]
    pick_built = sem("pick_built")
    tiles_summed = sem("tiles_summed")
    sums_copied = sem("sums_copied")
    st_turned = sem("st_turned")
    st_copied = sem("st_copied")
    xt_turned = sem("xt_turned")
    xt_copied = sem("xt_copied")
    h_done = sem("h_done")
    y_done = sem("y_done")
    stats_done = sem("stats_done")
    mean_var_done = sem("mean_var_done")
    std_done = sem("std_done")
    rstd_done = sem("rstd_done")
    norm_ready = sem("norm_ready")
    result_done = sem("result_done")
    stored = [sem(f"stored{i}") for i in range(DEEP)]

    def tiles_of(tau):
        return (1, LAST_ROWS) if isinstance(tau, int) and tau == TRIOS - 1 else (TRIO, P)

    def rows_of(dram, tau):
        tiles, rows = tiles_of(tau)
        if tiles == 1:
            return dram[NODES - rows:NODES, :].rearrange("(t p) d -> p t d", t=1)
        return dram[bass.ds(tau * (TRIO * P), TRIO * P), :].rearrange("(t p) d -> p t d", t=TRIO)


    def load_table(engine, tau, tiles):
        registers = [engine.alloc_register(nc.get_next_instruction_name().replace("I-", "word")) for _ in range(TRIO_TABLE)]
        engine.load(registers, table_row[:].rearrange("a e w -> a (e w)")[:, bass.ds(tau * TRIO_TABLE, TRIO_TABLE)])
        return [registers[q * TABLE:(q + 1) * TABLE] for q in range(TRIO)] + [registers[-1:]]

    def free_table(engine, table_registers):
        for register in sum(table_registers, []):
            engine.free_register(register)

    with nc.Block() as block_:
        @block_.sync
        def _(sp):
            sp.dma_start(edge_src[:], src.rearrange("(p e) -> p e", p=EDGE_ROWS)).then_inc(edges_landed, 16)
            sp.dma_start(edge_dst[:, 0:EDGE_COLS], dst.rearrange("(p e) -> p e", p=EDGE_ROWS)).then_inc(edges_landed, 16)
            sp.wait_ge(next_set, 1)
            sp.dma_start(edge_dst[0:EDGE_ROWS - 1, EDGE_COLS:EDGE_COLS + 1],
                         dst.rearrange("(p e) -> p e", p=EDGE_ROWS)[1:EDGE_ROWS, 0:1],
                         allow_slow_non_contiguous=True).then_inc(next_landed, 16)
            sp.dma_start(k.ws[:], w_self).then_inc(k.weights_landed, 16)
            sp.dma_start(k.wn[:], w_neigh).then_inc(k.weights_landed, 16)
            sp.dma_start(k.bs_row[:], b_self.rearrange("(a d) -> a d", a=1)).then_inc(k.weights_landed, 16)
            sp.dma_start(k.bn_row[:], b_neigh.rearrange("(a d) -> a d", a=1)).then_inc(k.weights_landed, 16)
            sp.dma_start(k.bn[:], b_neigh.rearrange("(a d) -> a d", a=1).partition_broadcast(P)).then_inc(k.bn_landed, 16)
            sp.wait_ge(pads_set, 1)
            sp.dma_start(words_padded[EDGES:EDGES + PAD, :].rearrange("e o -> o e"), pad_words[:]).then_inc(padded_stored, 16)
            for tau in range(DEEP):
                sp.dma_start(x_in[tau][:], rows_of(x, tau)).then_inc(x_landed[tau], 16)
            sp.wait_ge(ends_done, 1)
            sp.dma_start(ends_dram[0, :].rearrange("(p w) -> p w", p=EDGE_ROWS), ends[:].rearrange("p a b -> p (a b)")).then_inc(ends_stored, 16)
            sp.wait_ge(upto_done, 1)
            sp.dma_start(kept_upto_dram.rearrange("(p b) e -> p (b e)", p=EDGE_ROWS), kept_upto[:]).then_inc(upto_stored, 16)
            sp.wait_ge(ends_stored, 16)
            sp.dma_start(all_ends[:].rearrange("p a b c -> p (a b c)"), ends_dram.partition_broadcast(SPREAD)).then_inc(ends_landed, 16)
            sp.wait_ge(words_done, 1)
            sp.dma_start(words_padded[0:EDGES, :].rearrange("(p e) o -> p (e o)", p=EDGE_ROWS), edge_words[:]).then_inc(padded_stored, 16)
            sp.wait_ge(k.parts_made, 3)
            for q in range(TRIO):
                sp.dma_start(k.bias[q * PARTS:(q + 1) * PARTS, q, :], k.bias_part[:, :, 0, :]).then_inc(k.parts_landed, 16)
                sp.dma_start(k.bias[TRIO * PARTS:BIAS_ROWS, q, :], k.bias_part[:, :, 1, :]).then_inc(k.parts_landed, 16)
            sp.wait_ge(table_done, 1)
            for mine, dram in ((table, table_dram), (bounds, bounds_dram)):
                sp.dma_start(dram.rearrange("(j p) w -> p j w", p=SPREAD), mine[:]).then_inc(table_stored, 16)
            sp.wait_ge(table_stored, 32)
            sp.dma_start(bounds_row[:].rearrange("a e w -> a (e w)"),
                         bounds_dram.rearrange("e w -> (e w)").rearrange("(a w) -> a w", a=1)).then_inc(table_landed, 16)
            whole = TILES // TRIO * TRIO
            sp.dma_start(table_row[:, 0:whole // TRIO, 0:TRIO * TABLE],
                         table_dram[0:whole, :].rearrange("(a n q) w -> a n (q w)", a=1, q=TRIO)).then_inc(table_landed, 16)
            sp.wait_ge(next_set, 2)
            sp.dma_start(table_row[:, whole // TRIO, 0:(TILES - whole) * TABLE],
                         table_dram[whole:TILES, :].rearrange("(a q) w -> a (q w)", a=1)).then_inc(table_landed, 16)

            def load_x(t, u):
                tau = t + u
                sp.wait_ge(y_done, tau - DEEP + 1)
                sp.dma_start(x_in[u % DEEP][0:tiles_of(tau)[1], 0:tiles_of(tau)[0], :], rows_of(x, tau)).then_inc(x_landed[u % DEEP], 16)

            def store(t, u):
                tau = t + u
                tiles, rows = tiles_of(tau)
                sp.wait_ge(result_done, tau + 1)
                sp.dma_start(rows_of(out, tau), result[u % DEEP][0:rows, 0:tiles, :]).then_inc(stored[u % DEEP], 16)

            def step(t, u):
                tau = t + u
                known = isinstance(tau, int)
                if not known or tau < TRIOS:
                    load_x(t, u)
                if not known or tau >= DEEP + 2:
                    store(t, u - DEEP - 2)

            for u in range(DEEP):
                step(DEEP, u)
            with sp.Fori(START, LOOPED - DEEP + 1, DEEP) as t:
                for u in range(DEEP):
                    step(t, u)
            for u in range(TRIOS + DEEP + 2 - LOOPED):
                step(LOOPED, u)
            for i in range(DEEP):
                sp.wait_ge(stored[i], 16 * len(range(i, TRIOS, DEEP)))

        @block_.gpsimd
        def _(pool):
            def iota(out_, pattern, multiplier):
                return nc.gpsimd.iota(out_, pattern, base=0, channel_multiplier=multiplier, allow_small_or_imprecise_dtypes=True)

            iota(k.column[:], [[1, P]], 0).then_inc(k.iotas, 1)
            iota(k.partition[:], [[1, 1]], 1).then_inc(k.iotas, 1)
            iota(limit[:], [[P * SPREAD, COLUMNS]], P).then_inc(k.iotas, 1)
            iota(entry[:], [[SPREAD, COLUMNS]], 1).then_inc(k.iotas, 1)
            iota(column3[:], [[0, SPAN], [1, P]], 0).then_inc(k.iotas, 1)
            iota(tile_base[:], [[P, TILES]], 0).then_inc(k.iotas, 1)
            nc.gpsimd.memset(ring[:, :, DIM:DIM + PARTS], 1.0).then_inc(ones_set, 1)
            pool.wait_ge(upto_stored, 16)

            def load_kept_blocks(js):
                for j in js:
                    nc.gpsimd.indirect_dma_start(kept_block[:, j, :], None, kept_upto_dram,
                                                 bass.IndirectOffsetOnAxis(ap=block_index[:, 0, j:j + 1], axis=0)
                                                 ).then_inc(block_landed[j], 16)

            def load_windows(js):
                for j in js:
                    nc.gpsimd.indirect_dma_start(window[0][:, j, :], None, words_padded,
                                                 bass.IndirectOffsetOnAxis(ap=place_index[:, 0, j:j + 1], axis=0)
                                                 ).then_inc(window_landed[j], 16)

            pool.wait_ge(blocks_found, 1)
            load_kept_blocks([0])
            pool.wait_ge(blocks_found, 2)
            load_kept_blocks(range(1, COLUMNS))
            pool.wait_ge(padded_stored, 32)
            pool.wait_ge(places_found, 1)
            load_windows([0])
            pool.wait_ge(blocks_found, 3)
            for j in range(COLUMNS):
                nc.gpsimd.indirect_dma_start(dst_block[:, j, :], None, dst.rearrange("(b e) -> b e", e=BLOCK),
                                             bass.IndirectOffsetOnAxis(ap=block_index[:, 1, j:j + 1], axis=0)
                                             ).then_inc(block_landed[COLUMNS + j], 16)
            pool.wait_ge(places_found, 2)
            load_windows(range(1, COLUMNS))

            def gather(r, slot):
                round_ = slot // GATHER_SEMS
                if not (isinstance(r, int) and r == 0 and round_ == 0):
                    pool.wait_ge(gathered[slot % GATHER_SEMS], r * (16 * (RING // GATHER_SEMS)) + 16 * round_)
                    pool.sem_inc(slots_free, 1)
                nc.gpsimd.indirect_dma_start(ring[:, slot, 0:DIM], None, x,
                                             bass.IndirectOffsetOnAxis(ap=staged[:, slot:slot + 1], axis=0)
                                             ).then_inc(gathered[slot % GATHER_SEMS], 16)

            def stage(r, h, count):
                if not (isinstance(r, int) and r == 0):
                    pool.wait_ge(tiles_summed, r * RING + (h * STAGE + STAGE - 1 - RING + DRIFT + 1))
                nc.gpsimd.tensor_copy(staged[:, h * STAGE:h * STAGE + count],
                                      chunk_src[:, bass.ds(r * RING + h * STAGE, count)]).then_inc(stage_done, 1)
                pool.wait_ge(stage_done, r * (RING // STAGE) + h + 1)
                for slot in range(h * STAGE, h * STAGE + count):
                    gather(r, slot)

            pool.wait_ge(chunks_known, 2)
            for h in range(RING // STAGE):
                stage(0, h, STAGE)
            pool.wait_ge(chunks_known, 4)
            with pool.Fori(1, CHUNKS // RING, 1) as r:
                for h in range(RING // STAGE):
                    stage(r, h, STAGE)
            stage(CHUNKS // RING, 0, CHUNKS % RING)

        @block_.vector
        def _(dve):
            chain = [0]

            def link(ins):
                chain[0] += 1
                ins.then_inc(dve_order, 1)
                dve.wait_ge(dve_order, chain[0])

            v = nc.vector
            v.memset(edge_dst[:, EDGE_COLS:EDGE_COLS + 1], NO_NODE).then_inc(next_set, 1)
            v.memset(pad_words[:], NODES).then_inc(pads_set, 1)
            v.memset(table_row[:, TRIOS - 1:TRIOS, :], 0).then_inc(next_set, 1)
            v.memset(thirds[:], 0.0)
            v.memset(k.ones[:], 1.0)
            v.memset(k.eps[:], EPS)
            v.memset(zeros[:], 0.0)
            v.memset(checks[:], 0.0)
            v.memset(chunk_dst[:, ENTRIES:ENTRIES + 1], float(NO_NODE))
            v.memset(degrees_t[0][:], 1.0)
            v.memset(degrees_t[1][:], 1.0)
            link(v.memset(k.bias[:], 0.0))
            dve.wait_ge(k.iotas, 2)
            v.tensor_scalar(k.before[:], k.column[:], k.partition[:, 0:1], None, ALU.is_gt)
            v.tensor_scalar(k.identity[:], k.column[:], k.partition[:, 0:1], None, ALU.is_equal).then_inc(k.consts_made, 1)

            dve.wait_ge(edges_landed, 32)
            v.tensor_tensor(flag_a[:], edge_src[:], edge_dst[:, 0:EDGE_COLS], ALU.not_equal)
            dve.wait_ge(next_landed, 16)
            link(v.tensor_tensor(flag_b[:], edge_dst[:, 1:EDGE_COLS + 1], edge_dst[:, 0:EDGE_COLS], ALU.is_equal))
            link(v.tensor_tensor(flag_b[:], flag_a[:], flag_b[:], ALU.max))
            v.tensor_tensor_scan(kept_upto[:], flag_b[:], zeros[:], 0.0, ALU.add, ALU.add).then_inc(row_counts, 1)
            dve.wait_ge(rows_summed, 1)
            link(v.tensor_copy(rows_before[:], bank[0][0:EDGE_ROWS, 0:1]))
            link(v.tensor_copy(checks[0:EDGE_ROWS, 4:5], kept_upto[:, EDGE_COLS - 1:EDGE_COLS]))
            v.tensor_scalar(kept_upto[:], kept_upto[:], rows_before[:, 0:1], None, ALU.add).then_inc(upto_done, 1)
            dve.wait_ge(upto_done, 1)
            v.tensor_copy(ends[:, 0, :], kept_upto[:, BLOCK - 1:EDGE_COLS:BLOCK])
            v.tensor_copy(ends[:, 1, :], edge_dst[:, BLOCK - 1:EDGE_COLS:BLOCK]).then_inc(ends_done, 1)
            link(v.tensor_tensor(dst_if_kept[:], edge_dst[:, 0:EDGE_COLS], flag_b[:], ALU.mult))
            v.scalar_tensor_tensor(edge_words[:], edge_src[:], 16, dst_if_kept[:], ALU.logical_shift_left, ALU.bitwise_or).then_inc(words_done, 1)
            dve.wait_ge(k.weights_landed, 64)
            v.tensor_tensor(k.wsum[:], k.ws[:], k.wn[:], ALU.add).then_inc(k.consts_made, 1)
            v.tensor_copy(k.bias_row[:, 0, :], k.bn_row[:])
            link(v.tensor_tensor(k.bias_row[:, 1, :], k.bs_row[:], k.bn_row[:], ALU.add))
            v.tensor_copy(k.bias_part[:, 0, :, :], k.bias_row[:]).then_inc(k.parts_made, 1)
            dve.wait_ge(k.parts_made, 1)
            link(v.tensor_tensor(k.bias_rest[:, 0, :, :], k.bias_row[:], k.bias_part[:, 0, :, :], ALU.subtract))
            v.tensor_copy(k.bias_part[:, 1, :, :], k.bias_rest[:, 0, :, :]).then_inc(k.parts_made, 1)
            dve.wait_ge(k.parts_made, 2)
            link(v.tensor_tensor(k.bias_rest[:, 1, :, :], k.bias_rest[:, 0, :, :], k.bias_part[:, 1, :, :], ALU.subtract))
            v.tensor_copy(k.bias_part[:, 2, :, :], k.bias_rest[:, 1, :, :]).then_inc(k.parts_made, 1)

            v.tensor_tensor(flag_a[:], edge_dst[:, 1:EDGE_COLS + 1], edge_dst[:, 0:EDGE_COLS], ALU.is_lt)
            dve.wait_ge(ends_landed, 16)
            dve.wait_ge(k.iotas, 6)
            def find_blocks(a, j0, j1):
                for j in range(j0, j1):
                    ins = v.tensor_scalar(below[j][:].rearrange("p (a b) -> p a b", a=EDGE_ROWS), all_ends[:, :, a, :],
                                          limit[:, j:j + 1], 0.0, (ALU.is_le, ALU.is_lt)[a], ALU.add, accum_out=counts[:, a, j:j + 1])
                link(ins)
                link(v.tensor_scalar(block[:, a, j0:j1], counts[:, a, j0:j1], float(BLOCKS - 1), None, ALU.min))
                v.tensor_copy(block_index[:, a, j0:j1], block[:, a, j0:j1]).then_inc(blocks_found, 1)

            def find_places(a, j0, j1):
                for j in range(j0, j1):
                    dve.wait_ge(block_landed[a * COLUMNS + j], 16)
                    ins = v.tensor_scalar(below[j][:, 0:BLOCK], (kept_block, dst_block)[a][:, j, :], limit[:, j:j + 1], 0.0,
                                          (ALU.is_le, ALU.is_lt)[a], ALU.add, accum_out=in_block[:, a, j:j + 1])
                link(ins)
                link(v.scalar_tensor_tensor(place[:, a, j0:j1], block[:, a, j0:j1], float(BLOCK), in_block[:, a, j0:j1], ALU.mult, ALU.add))
                v.tensor_copy(place_index[:, a, j0:j1], place[:, a, j0:j1]).then_inc(places_found, 1)

            find_blocks(0, 0, 1)
            find_blocks(0, 1, COLUMNS)
            find_places(0, 0, 1)
            find_blocks(1, 0, COLUMNS)
            find_places(0, 1, COLUMNS)

            def pack_start(j0, j1):
                js = slice(j0, j1)
                for j in range(j0, j1):
                    dve.wait_ge(window_landed[j], 16)
                link(v.tensor_scalar(low[:, js, :], window[0][:, js, :], 0xFFFF, None, ALU.bitwise_and))
                link(v.tensor_copy(first_dst[:, js], low[:, js, 0]))
                for j in range(j0, j1):
                    ins = v.tensor_scalar(moves[:, j, :], low[:, j, :], first_dst[:, j:j + 1], 0.0, ALU.subtract, ALU.max)
                link(ins)
                link(v.scalar_tensor_tensor(window[1][:, js, :], window[0][:, js, :], HIGH_BITS, moves[:, js, :],
                                            ALU.bitwise_and, ALU.bitwise_or))

            def pack_bits(j0, j1, bits):
                js = slice(j0, j1)
                for bit in bits:
                    step = 1 << bit
                    old, new = 1 - bit % 2, bit % 2
                    put = min(WINDOW, P + (1 << SHIFT_BITS) - 2 * step)
                    read = min(WINDOW, put + step)
                    link(v.tensor_scalar(moves[:, js, 0:read], window[old][:, js, 0:read], 31 - bit, 31,
                                         ALU.logical_shift_left, ALU.arith_shift_right))
                    link(v.scalar_tensor_tensor(window[new][:, js, 0:put], moves[:, js, 0:put], -1, window[old][:, js, 0:put],
                                                ALU.bitwise_xor, ALU.bitwise_and))
                    link(v.copy_predicated(window[new][:, js, 0:read - step], moves[:, js, step:read], window[old][:, js, step:read]))

            def pack_end(j0, j1):
                js = slice(j0, j1)
                final = window[1 - SHIFT_BITS % 2]
                v.tensor_scalar(pair_field[:, 0, js, :], final[:, js, 0:P], 16, None, ALU.logical_shift_right)
                link(v.tensor_scalar(pair_field[:, 1, js, :], final[:, js, 0:P], 0xFFFF, None, ALU.bitwise_and))
                for j in range(j0, j1):
                    v.tensor_scalar(pair_value[:, 1, j, :], pair_field[:, 1, j, :], first_dst[:, j:j + 1], None, ALU.add)
                v.tensor_copy(pair_value[:, 0, js, :], pair_field[:, 0, js, :]).then_inc(fields_done, 1)

            pack_start(0, 1)
            pack_bits(0, 1, range(SHIFT_BITS))
            pack_end(0, 1)
            dve.wait_ge(fields_turned, 1)
            v.tensor_copy(chunk_src[:, 0:SPREAD], bank[0][:, 0:SPREAD]).then_inc(chunks_known, 1)
            v.tensor_copy(chunk_dst[:, 0:SPREAD], bank[0][:, SPREAD:2 * SPREAD]).then_inc(chunks_known, 1)
            find_places(1, 0, COLUMNS)

            link(v.tensor_tensor(packed_before[:], place[:, 1, :], limit[:], ALU.subtract))
            dve.wait_ge(places_found, 3)
            link(v.tensor_scalar(first_int[:], place_index[:, 1, :], 7, None, ALU.logical_shift_right))
            link(v.tensor_copy(first[:], first_int[:]))
            link(v.tensor_tensor(first[:], first[:], entry[:], ALU.subtract))
            link(v.tensor_tensor(drift[:], first[:], entry[:], ALU.subtract))
            link(v.tensor_scalar(drift_in[:], drift[:], float(-DRIFT), float(DRIFT), ALU.max, ALU.min))
            link(v.tensor_tensor(first[:], drift_in[:], entry[:], ALU.add))
            link(v.tensor_scalar(first[:], first[:], 0.0, float(CHUNKS - 1), ALU.max, ALU.min))
            for s in range(SPAN):
                ins = v.tensor_scalar(ring_slot[:, s, :], first[:], float(s), None, ALU.add)
            link(ins)
            link(v.tensor_scalar(laps[1][:], ring_slot[:], float(RING), None, ALU.is_ge))
            top = (CHUNKS + SPAN) // RING
            for lap in range(2, top + 1):
                link(v.scalar_tensor_tensor(laps[lap % 2][:], ring_slot[:], float(RING * lap), laps[1 - lap % 2][:], ALU.is_ge, ALU.add))
            link(v.scalar_tensor_tensor(ring_slot[:], laps[top % 2][:], float(-RING), ring_slot[:], ALU.mult, ALU.add))
            for s in range(SPAN):
                v.tensor_scalar(table[:, :, s], ring_slot[:, s, :], float(ROW), None, ALU.mult)
            v.tensor_copy(table[:, :, SPAN], first[:])
            v.tensor_copy(bounds[:, :, 0], packed_before[:])
            v.tensor_copy(bounds[:, :, 2], place[:, 0, :])
            v.tensor_scalar(bounds[:, :, 1], first[:], float(P), float((SPAN - 1) * P), ALU.mult, ALU.add).then_inc(table_done, 1)

            pack_start(1, COLUMNS)
            pack_bits(1, COLUMNS, range(0, 1))
            dve.wait_ge(table_landed, 48)
            link(v.tensor_tensor(thirds[:, 0:TILES], bounds_row[:, 1:TILES + 1, 0], bounds_row[:, 0:TILES, 1], ALU.is_gt))
            link(v.reduce_sum(trio_thirds[:], thirds[:].rearrange("a (t q) -> a t q", q=TRIO), AXIS_X))
            v.tensor_copy(table_row[:, :, TRIO_TABLE - 1], trio_thirds[:]).then_inc(thirds_done, 1)
            def check():
                v.reduce_sum(checks[0:EDGE_ROWS, 0:1], flag_a[:], AXIS_X)
                link(v.tensor_tensor(drift_out[:], drift[:], drift_in[:], ALU.not_equal))
                v.reduce_sum(checks[0:SPREAD, 2:3], drift_out[:], AXIS_X)
                link(v.scalar_tensor_tensor(cover[:], bounds_row[:, 0:TILES, 1], float(P * (SPAN - 2)), bounds_row[:, 1:TILES + 1, 0],
                                            ALU.add, ALU.is_lt))
                v.reduce_sum(check_all[:, 1:2], cover[:], AXIS_X)
                link(v.tensor_tensor(length, bounds_row[:, 1:CHUNKS + 1, 2], bounds_row[:, 0:CHUNKS, 2], ALU.subtract))
                link(v.tensor_scalar(too_long, length, float(WINDOW), None, ALU.is_gt))
                link(v.reduce_sum(check_all[:, 2:3], too_long, AXIS_X))
                v.tensor_copy(checks[0:1, 1:2], check_all[:, 1:2])
                v.tensor_copy(checks[0:1, 3:4], check_all[:, 2:3]).then_inc(checks_done, 1)

            def conclude():
                v.tensor_scalar(degrees[:], degrees[:], float(MAX_DEGREE), 0.0, ALU.is_gt, ALU.add,
                                accum_out=checks[:, 5:6]).then_inc(checks_done, 1)
                dve.wait_ge(checks_summed, 1)
                link(v.tensor_copy(check_sums[:], sum_bank[0][0:1, 0:6]))
                link(v.tensor_scalar(check_sums[:, 4:5], check_sums[:, 4:5], float(PACKED), None, ALU.not_equal))
                link(v.reduce_sum(check_all[:, 0:1], check_sums[:], AXIS_X))
                link(v.tensor_scalar(k.needs_general[:], check_all[:, 0:1], 0.0, None, ALU.is_gt))

            def load_words(t, u):
                return load_table(dve, t + u, tiles_of(t + u)[0])

            def pick_chunks(t, u, words, tiles, s0, s1):
                for q in tiles:
                    n = (t + u) * TRIO + q
                    first_chunk = dve.snap(words[q][SPAN], min_val=0, max_val=CHUNKS - 1)
                    ins = v.scalar_tensor_tensor(pick[u % DEEP][:, q, s0:s1, :], column3[:, s0:s1, :], tile_base[:, bass.ds(n, 1)],
                                                 chunk_dst[:, bass.ds(first_chunk + s0, s1 - s0)].unsqueeze(2).to_broadcast([P, s1 - s0, P]),
                                                 ALU.add, ALU.is_equal)
                return ins

            def pick_tile(t, u, words, q):
                tau = t + u
                if q == 0 and not (isinstance(tau, int) and tau < DEEP):
                    dve.wait_ge(tiles_summed, (tau - (DEEP - 1)) * TRIO)
                if q < tiles_of(tau)[0] - 1:
                    pick_chunks(t, u, words, [q], 0, SPAN - 1)

            def last_picks(t, u, words):
                tiles = tiles_of(t + u)[0]
                with dve.If(dve.snap(words[TRIO][0], min_val=0, max_val=TRIO) > 0):
                    pick_chunks(t, u, words, range(tiles), SPAN - 1, SPAN)
                pick_chunks(t, u, words, range(tiles - 1, tiles), 0, SPAN - 1).then_inc(pick_built, 1)
                free_table(dve, words)

            def residual(t, u):
                tau, b = t + u, u % 2
                tiles, rows = tiles_of(tau)
                dve.wait_ge(h_done, tau + 1)
                if not (isinstance(tau, int) and tau < DEEP):
                    dve.wait_ge(result_done, tau - (DEEP - 1))
                v.scalar_tensor_tensor(y[u % DEEP][0:rows, 0:tiles, :],
                                       h_bank[b][0:rows, 0:tiles * DIM].rearrange("p (q d) -> p q d", q=tiles), 0.0,
                                       x_in[u % DEEP][0:rows, 0:tiles, :], ALU.max, ALU.add).then_inc(y_done, 1)
                v.tensor_copy(degrees[:, bass.ds(tau * TRIO, tiles)], degrees_n[u % DEEP][:, 0:tiles * PARTS:PARTS])

            def statistics(t, u):
                tau, b = t + u, u % DEEP
                tiles, rows = tiles_of(tau)
                dve.wait_ge(y_done, tau + 1)
                for q in range(tiles):
                    ins = v.bn_stats(stats[b][0:rows, q, :], y[b][0:rows, q, :])
                ins.then_inc(stats_done, 1)

            def aggregate(t, u):
                tau, b = t + u, u % DEEP
                tiles, rows = tiles_of(tau)
                for q in range(tiles):
                    ins = v.bn_aggr(mean_var[b][0:rows, q, :], stats[b][0:rows, q, :])
                ins.then_inc(mean_var_done, 1)

            def invert(t, u):
                tau, b = t + u, u % DEEP
                tiles, rows = tiles_of(tau)
                if not (isinstance(tau, int) and tau + 1 >= TRIOS):
                    dve.wait_ge(stats_done, tau + 2)
                dve.wait_ge(std_done, tau + 1)
                v.reciprocal(rstd[b][0:rows, 0:tiles], std[b][0:rows, 0:tiles]).then_inc(rstd_done, 1)

            def scale_mean(t, u):
                tau, b = t + u, u % DEEP
                tiles, rows = tiles_of(tau)
                dve.wait_ge(rstd_done, tau + 1)
                v.scalar_tensor_tensor(minus_mean[b][0:rows, 0:tiles], mean_var[b][0:rows, 0:tiles, 0], -1.0,
                                       rstd[b][0:rows, 0:tiles], ALU.mult, ALU.mult).then_inc(norm_ready, 1)

            def step(t, u):
                tau = t + u
                known = isinstance(tau, int)
                picks = not known or tau + 3 < TRIOS
                rest = not known or 1 <= tau <= TRIOS
                scaling = not known or 2 <= tau < TRIOS + 2
                if rest:
                    residual(t, u - 1)
                if picks:
                    words = load_words(t, u + 3)
                    pick_tile(t, u + 3, words, 0)
                if rest:
                    statistics(t, u - 1)
                if picks:
                    pick_tile(t, u + 3, words, 1)
                    last_picks(t, u + 3, words)
                if known and tau == 1:
                    dve.wait_ge(stats_done, 1)
                if scaling:
                    invert(t, u - 2)
                if rest:
                    aggregate(t, u - 1)
                if scaling:
                    scale_mean(t, u - 2)

            dve.wait_ge(k.bn_landed, 16)
            dve.wait_ge(thirds_done, 1)
            dve.wait_ge(chunks_known, 2)
            for u in range(3):
                words = load_words(0, u)
                pick_tile(0, u, words, 0)
                pick_tile(0, u, words, 1)
                last_picks(0, u, words)
            for u in range(START):
                if 1 + u < SHIFT_BITS:
                    pack_bits(1, COLUMNS, range(1 + u, 2 + u))
                if 1 + u == SHIFT_BITS:
                    pack_end(1, COLUMNS)
                step(0, u)
            dve.wait_ge(fields_turned, 2)
            v.tensor_copy(chunk_src[:, SPREAD:ENTRIES], bank[0][:, 0:ENTRIES - SPREAD]).then_inc(chunks_known, 1)
            v.tensor_copy(chunk_dst[:, SPREAD:ENTRIES], bank[1][:, 0:ENTRIES - SPREAD]).then_inc(chunks_known, 1)
            dve.wait_ge(chunks_known, 4)

            with dve.Fori(START, LOOPED - UNROLL + 1, UNROLL) as t:
                for u in range(UNROLL):
                    step(t, u)
            check()
            for u in range(TRIOS + 2 - LOOPED):
                step(LOOPED, u)
            conclude()

        @block_.tensor
        def _(pe):
            mm = nc.tensor.matmul
            pe.wait_ge(k.consts_made, 1)
            pe.wait_ge(row_counts, 1)
            mm(bank[0][0:EDGE_ROWS, 0:1], k.before[0:EDGE_ROWS, 0:EDGE_ROWS], kept_upto[:, EDGE_COLS - 1:EDGE_COLS],
               start=True, stop=True).then_inc(rows_summed, 1)
            pe.wait_ge(k.consts_made, 2)
            for i, w in enumerate((k.ws, k.wn, k.wsum)):
                nc.tensor.transpose(bank[2 + i][:, 0:P], w[:], k.identity[:]).then_inc(k.weights_turned, 1)
            pe.wait_ge(fields_done, 1)
            nc.tensor.transpose(bank[0][:, 0:SPREAD], pair_value[:, 0, 0, :], k.identity[0:SPREAD, 0:SPREAD])
            nc.tensor.transpose(bank[0][:, SPREAD:2 * SPREAD], pair_value[:, 1, 0, :],
                                k.identity[0:SPREAD, 0:SPREAD]).then_inc(fields_turned, 1)

            def turn_x(t, u):
                tau, b = t + u, u % 2
                tiles, rows = tiles_of(tau)
                pe.wait_ge(x_landed[u % DEEP], 4 * (t + u // DEEP * DEEP) + 16)
                if not (isinstance(tau, int) and tau < 2):
                    pe.wait_ge(xt_copied, tau - 1)
                for q in range(tiles):
                    ins = nc.tensor.transpose(xt_bank[b][:, q * P:q * P + rows], x_in[u % DEEP][0:rows, q, :], k.identity[0:rows, 0:rows])
                ins.then_inc(xt_turned, 1)

            def sum_rows(t, u):
                tau, b = t + u, u % 2
                known = isinstance(tau, int)
                pe.wait_ge(pick_built, tau + 1)
                if not known or tau >= 2:
                    pe.wait_ge(sums_copied, tau - 1)
                tiles, _ = tiles_of(tau)
                words = load_table(pe, tau, tiles)

                def chunk_product(q, s):
                    slot = pe.snap(words[q][s], min_val=0, max_val=(RING - 1) * ROW)
                    return mm(sum_bank[b][:, q * ROW:q * ROW + DIM + PARTS], pick[u % DEEP][:, q, s, :],
                              ring[:].rearrange("p c w -> p (c w)")[:, bass.ds(slot, DIM + PARTS)],
                              start=(q == 0 and s == 0), stop=(q == tiles - 1 and s == 1))

                for q in range(tiles):
                    ahead = u * TRIO + q + DRIFT + SPAN - 1
                    n = tau * TRIO + q
                    if known and tau == 0 and q == 0:
                        for c in range(ahead):
                            pe.wait_ge(gathered[c % GATHER_SEMS], 16)
                    if not known or n + DRIFT + SPAN - 1 < CHUNKS:
                        pe.wait_ge(gathered[ahead % GATHER_SEMS], 4 * t + 16 * (ahead // GATHER_SEMS + 1))
                    chunk_product(q, 0)
                with pe.If(pe.snap(words[TRIO][0], min_val=0, max_val=TRIO) > 0):
                    for q in range(tiles):
                        chunk_product(q, 2)
                for q in range(tiles):
                    chunk_product(q, 1).then_inc(tiles_summed, 1)
                free_table(pe, words)

            def turn_sums(t, u):
                tau, b = t + u, u % 2
                pe.wait_ge(sums_copied, tau + 1)
                if not (isinstance(tau, int) and tau < 2):
                    pe.wait_ge(st_copied, tau - 1)
                tiles, _ = tiles_of(tau)
                for q in range(tiles):
                    nc.tensor.transpose(st_bank[b][:, q * P:q * P + P], sums[u % DEEP][:, q, 0:DIM], k.identity[:])
                nc.tensor.transpose(st_bank[b][0:tiles * PARTS, TRIO * P:TRIO * P + P], degrees_n[u % DEEP][:, 0:tiles * PARTS],
                                    k.identity[:]).then_inc(st_turned, 1)

            def products(t, u):
                tau, b = t + u, u % 2
                tiles, rows = tiles_of(tau)
                pe.wait_ge(st_copied, tau + 1)
                pe.wait_ge(xt_copied, tau + 1)
                if not (isinstance(tau, int) and tau < 2):
                    pe.wait_ge(y_done, tau - 1)
                mm(h_bank[b][0:rows, 0:tiles * DIM], degrees_t[b][:, 0:rows], k.bias[:, 0:tiles, :].rearrange("k q d -> k (q d)"),
                   start=True, stop=False)
                for q in range(tiles):
                    h = h_bank[b][0:rows, q * DIM:q * DIM + DIM]
                    mm(h, x_t[b][:, q, 0:rows], k.wsum_t[:], start=False, stop=False)
                    ins = mm(h, sums_t[b][:, q, 0:rows], k.wn_t[:], start=False, stop=(q == tiles - 1))
                ins.then_inc(h_done, 1)

            def step(t, u):
                tau = t + u
                known = isinstance(tau, int)
                turn_sums(t, u)
                if not known or tau + 1 < TRIOS:
                    sum_rows(t, u + 1)
                    turn_x(t, u + 1)
                products(t, u)

            pe.wait_ge(k.weights_copied, 3)
            pe.wait_ge(k.parts_landed, 16 * 2 * TRIO)
            pe.wait_ge(table_landed, 48)
            pe.wait_ge(thirds_done, 1)
            pe.wait_ge(ones_set, 1)
            turn_x(0, 0)
            sum_rows(0, 0)
            for u in range(START):
                step(0, u)
            pe.wait_ge(fields_done, 2)
            pe.wait_ge(sums_copied, START + 1)
            for a in range(2):
                for j in range(1, COLUMNS):
                    ins = nc.tensor.transpose(bank[a][:, (j - 1) * SPREAD:j * SPREAD], pair_value[:, a, j, :],
                                              k.identity[0:SPREAD, 0:SPREAD])
            ins.then_inc(fields_turned, 1)
            pe.wait_ge(chunks_known, 4)
            with pe.Fori(START, LOOPED - UNROLL + 1, UNROLL) as t:
                for u in range(UNROLL):
                    step(t, u)
            for u in range(TRIOS - LOOPED):
                step(LOOPED, u)
            pe.wait_ge(checks_done, 2)
            pe.wait_ge(sums_copied, TRIOS)
            mm(sum_bank[0][0:1, 0:6], k.ones[:, 0:1], checks[:], start=True, stop=True).then_inc(checks_summed, 1)

        @block_.scalar
        def _(act):
            for i, w_t in enumerate((k.ws_t, k.wn_t, k.wsum_t)):
                act.wait_ge(k.weights_turned, i + 1)
                nc.scalar.copy(w_t[:], bank[2 + i][:, 0:P]).then_inc(k.weights_copied, 1)

            def copy_sums(t, u):
                tau, b = t + u, u % 2
                tiles, _ = tiles_of(tau)
                act.wait_ge(tiles_summed, tau * TRIO + tiles)
                summed = sum_bank[b][:, 0:TRIO * ROW].rearrange("p (q w) -> p q w", q=TRIO)
                nc.scalar.copy(sums[u % DEEP][:, 0:tiles, :], summed[:, 0:tiles, 0:DIM])
                nc.scalar.copy(degrees_n[u % DEEP][:, 0:tiles * PARTS].rearrange("p (q w) -> p q w", q=tiles),
                               summed[:, 0:tiles, DIM:DIM + PARTS]).then_inc(sums_copied, 1)

            def copy_sums_t(t, u):
                tau, b = t + u, u % 2
                tiles, _ = tiles_of(tau)
                act.wait_ge(st_turned, tau + 1)
                nc.scalar.copy(sums_t[b][:, 0:tiles, :], st_bank[b][:, 0:tiles * P].rearrange("p (q w) -> p q w", q=tiles))
                nc.scalar.copy(degrees_t[b][0:tiles * PARTS, :], st_bank[b][0:tiles * PARTS, TRIO * P:TRIO * P + P]).then_inc(st_copied, 1)

            def copy_x_t(t, u):
                tau, b = t + u, u % 2
                tiles, rows = tiles_of(tau)
                act.wait_ge(xt_turned, tau + 1)
                nc.scalar.copy(x_t[b][:, 0:tiles, 0:rows],
                               xt_bank[b][:, 0:tiles * P].rearrange("p (q w) -> p q w", q=tiles)[:, :, 0:rows]
                               ).then_inc(xt_copied, 1)

            def deviation(t, u):
                tau, b = t + u, u % DEEP
                tiles, rows = tiles_of(tau)
                act.wait_ge(mean_var_done, tau + 1)
                nc.scalar.activation(std[b][0:rows, 0:tiles], mean_var[b][0:rows, 0:tiles, 1], ACT.Sqrt,
                                     bias=k.eps[0:rows, 0:1], scale=1.0).then_inc(std_done, 1)

            def normalise(t, u):
                tau, b = t + u, u % DEEP
                tiles, rows = tiles_of(tau)
                act.wait_ge(norm_ready, tau + 1)
                if not (isinstance(tau, int) and tau < DEEP):
                    act.wait_ge(stored[b], 4 * (t + u // DEEP * DEEP))
                for q in range(tiles):
                    ins = nc.scalar.activation(result[b][0:rows, q, :], y[b][0:rows, q, :], ACT.Identity,
                                               bias=minus_mean[b][0:rows, q:q + 1], scale=rstd[b][0:rows, q:q + 1])
                ins.then_inc(result_done, 1)

            def step(t, u):
                tau = t + u
                known = isinstance(tau, int)
                if not known or tau < TRIOS:
                    copy_sums_t(t, u)
                if not known or 2 <= tau < TRIOS + 2:
                    deviation(t, u - 2)
                if not known or tau >= 3:
                    normalise(t, u - 3)
                if not known or tau + 1 < TRIOS:
                    copy_sums(t, u + 1)
                    copy_x_t(t, u + 1)

            copy_x_t(0, 0)
            copy_sums(0, 0)
            for u in range(START):
                step(0, u)
            with act.Fori(START, LOOPED - UNROLL + 1, UNROLL) as t:
                for u in range(UNROLL):
                    step(t, u)
            for u in range(TRIOS + 3 - LOOPED):
                step(LOOPED, u)


def build_general_case(nc, ctx, k, x, src, dst, out):
    def sb(name, shape, dtype=FP32):
        return ctx.enter_context(nc.sbuf_tensor(name, shape, dtype))

    def sem(name):
        return ctx.enter_context(nc.semaphore(name))

    sums_dram = nc.dram_tensor("sums_dram", (SUM_ROWS, ROW), FP32, kind="Internal").ap()
    zero_rows = sb("zero_rows", [P, ZERO_ROWS * ROW])
    bs = sb("bs", [P, DIM])
    dst_line = sb("dst_line", [GEN_EDGES, GEN_EDGES], INT32)
    dst_own = sb("dst_own", [GEN_EDGES, 1], INT32)
    src_own = sb("src_own", [GEN_EDGES, 1], INT32)
    dst_value = sb("dst_value", [GEN_EDGES, 1])
    spare_row = sb("spare_row", [GEN_EDGES, 1])
    earlier = sb("earlier", [GEN_EDGES, GEN_EDGES])
    same = sb("same", [GEN_EDGES, GEN_EDGES])
    same_earlier = sb("same_earlier", [GEN_EDGES, GEN_EDGES])
    repeats = sb("repeats", [GEN_EDGES, 1])
    is_repeat = sb("is_repeat", [GEN_EDGES, 1])
    to_spare = sb("to_spare", [GEN_EDGES, 1])
    moved = sb("moved", [GEN_EDGES, 1])
    target = sb("target", [GEN_EDGES, 1], INT32)
    rows = sb("rows", [GEN_EDGES, ROW])
    totals = sb("totals", [GEN_EDGES, ROW])
    x_rows = sb("x_rows", [GEN_ROWS, DIM])
    sum_rows = sb("sum_rows", [GEN_ROWS, ROW])
    x_turned = sb("x_turned", [P, 2, GEN_ROWS])
    biased = sb("biased", [GEN_ROWS, DIM])
    before_relu = sb("before_relu", [GEN_ROWS, DIM])
    y = sb("gen_y", [GEN_ROWS, DIM])
    stats = sb("gen_stats", [GEN_ROWS, 6])
    mean_var = sb("gen_mean_var", [GEN_ROWS, 2])
    std = sb("gen_std", [GEN_ROWS, 1])
    rstd = sb("gen_rstd", [GEN_ROWS, 1])
    result = sb("gen_result", [GEN_ROWS, DIM])
    totals_bank = ctx.enter_context(nc.psum_tensor("totals_bank", [P, 512], FP32))
    turn_bank = ctx.enter_context(nc.psum_tensor("turn_bank", [P, 512], FP32))
    h_bank = ctx.enter_context(nc.psum_tensor("gen_h_bank", [P, 512], FP32))

    zeros_set = sem("gen_zeros_set")
    zeroed = sem("gen_zeroed")
    bs_landed = sem("gen_bs_landed")
    step_landed = sem("gen_step_landed")
    rows_wanted = sem("gen_rows_wanted")
    rows_landed = sem("gen_rows_landed")
    same_done = sem("gen_same_done")
    target_done = sem("gen_target_done")
    totals_done = sem("gen_totals_done")
    totals_copied = sem("gen_totals_copied")
    adds_wanted = sem("gen_adds_wanted")
    added = sem("gen_added")
    steps_ended = sem("gen_steps_ended")
    order = sem("gen_order")
    tile_landed = sem("gen_tile_landed")
    turned = sem("gen_turned")
    turned_copied = sem("gen_turned_copied")
    h_done = sem("gen_h_done")
    var_done = sem("gen_var_done")
    std_done = sem("gen_std_done")
    result_done = sem("gen_result_done")
    stored = sem("gen_stored")

    EDGE_LINKS = 9
    TILE_LINKS = 5

    def only_if_needed(engine, program):
        needed = engine.value_load(k.needs_general[0:1, 0:1], min_val=0, max_val=1)
        with engine.If(needed > 0):
            program(engine)
            engine.nop()
        with engine.Else():
            engine.nop()
        engine.nop()

    with nc.Block() as block:
        @block.sync
        def _(sp):
            def program(sp):
                sp.dma_start(bs[:], k.inputs[1].rearrange("(a d) -> a d", a=1).partition_broadcast(P)).then_inc(bs_landed, 16)
                sp.wait_ge(zeros_set, 1)
                zero_view = sums_dram.rearrange("(z p r) w -> z p (r w)", p=P, r=ZERO_ROWS)
                for z in range(SUM_ROWS // (P * ZERO_ROWS)):
                    sp.dma_start(zero_view[z, :, :], zero_rows[:]).then_inc(zeroed, 16)
                with sp.Fori(0, GEN_STEPS, 1) as s:
                    edges = bass.ds(s * GEN_EDGES, GEN_EDGES)
                    sp.dma_start(dst_line[:], dst[edges].rearrange("(a e) -> a e", a=1).partition_broadcast(GEN_EDGES)).then_inc(step_landed, 16)
                    sp.dma_start(dst_own[:], dst[edges].rearrange("(e a) -> e a", a=1)).then_inc(step_landed, 16)
                    sp.dma_start(src_own[:], src[edges].rearrange("(e a) -> e a", a=1)).then_inc(step_landed, 16)
                    sp.wait_ge(added, s * 16 + 16)
                    sp.sem_inc(steps_ended, 1)
                with sp.Fori(0, GEN_TILES, 1) as n:
                    nodes = bass.ds(n * GEN_ROWS, GEN_ROWS)
                    sp.dma_start(x_rows[:], x[nodes, :]).then_inc(tile_landed, 16)
                    sp.dma_start(sum_rows[:], sums_dram[nodes, :]).then_inc(tile_landed, 16)
                    sp.wait_ge(result_done, n + 1)
                    sp.sem_inc(steps_ended, 1)

            only_if_needed(sp, program)

        @block.gpsimd
        def _(pool):
            def program(pool):
                pool.wait_ge(zeroed, 16 * (SUM_ROWS // (P * ZERO_ROWS)))
                with pool.Fori(0, GEN_STEPS, 1) as s:
                    pool.wait_ge(step_landed, s * 48 + 48)
                    pool.sem_inc(rows_wanted, 1)
                    nc.gpsimd.indirect_dma_start(rows[:, 0:DIM], None, x,
                                                 bass.IndirectOffsetOnAxis(ap=src_own[:, 0:1], axis=0)).then_inc(rows_landed, 16)
                    pool.wait_ge(target_done, s + 1)
                    pool.wait_ge(totals_copied, s + 1)
                    pool.sem_inc(adds_wanted, 1)
                    nc.gpsimd.indirect_dma_start(sums_dram, bass.IndirectOffsetOnAxis(ap=target[:, 0:1], axis=0), totals[:], None,
                                                 compute_op=ALU.add).then_inc(added, 16)

            only_if_needed(pool, program)

        @block.vector
        def _(dve):
            def program(dve):
                v = nc.vector
                v.memset(zero_rows[:], 0.0).then_inc(zeros_set, 1)
                v.memset(rows[:, DIM:DIM + 1], 1.0)
                v.memset(rows[:, DIM + 1:ROW], 0.0)
                v.tensor_scalar(spare_row[:], k.partition[0:GEN_EDGES, :], float(NODES), None, ALU.add)
                v.tensor_scalar(earlier[:], k.column[0:GEN_EDGES, 0:GEN_EDGES], k.partition[0:GEN_EDGES, 0:1], None, ALU.is_lt).then_inc(zeros_set, 1)
                dve.wait_ge(zeros_set, 2)
                with dve.Fori(0, GEN_STEPS, 1) as s:
                    links = [0]

                    def link(ins):
                        links[0] += 1
                        ins.then_inc(order, 1)
                        dve.wait_ge(order, s * EDGE_LINKS + links[0])

                    dve.wait_ge(step_landed, s * 48 + 48)
                    link(v.tensor_copy(dst_value[:], dst_own[:]))
                    v.tensor_scalar(same[:], dst_line[:], dst_value[:, 0:1], None, ALU.is_equal).then_inc(same_done, 1)
                    dve.wait_ge(same_done, s + 1)
                    link(v.tensor_tensor(same_earlier[:], same[:], earlier[:], ALU.mult))
                    link(v.reduce_sum(repeats[:], same_earlier[:], AXIS_X))
                    link(v.tensor_scalar(is_repeat[:], repeats[:], 0.0, None, ALU.is_gt))
                    link(v.tensor_tensor(to_spare[:], spare_row[:], dst_value[:], ALU.subtract))
                    link(v.tensor_tensor(moved[:], to_spare[:], is_repeat[:], ALU.mult))
                    link(v.tensor_tensor(moved[:], moved[:], dst_value[:], ALU.add))
                    v.tensor_copy(target[:], moved[:]).then_inc(target_done, 1)
                    dve.wait_ge(target_done, s + 1)
                    dve.wait_ge(totals_done, s + 1)
                    link(v.tensor_copy(totals[:, 0:DIM], totals_bank[0:GEN_EDGES, 0:DIM]))
                    link(v.tensor_copy(totals[:, DIM:ROW], totals_bank[0:GEN_EDGES, DIM:ROW]))
                    dve.sem_inc(totals_copied, 1)
                dve.wait_ge(bs_landed, 16)
                with dve.Fori(0, GEN_TILES, 1) as n:
                    links = [0]

                    def link(ins):
                        links[0] += 1
                        ins.then_inc(order, 1)
                        dve.wait_ge(order, n * TILE_LINKS + (GEN_STEPS * EDGE_LINKS + links[0]))

                    dve.wait_ge(h_done, n + 1)
                    link(v.tensor_tensor(biased[:], bs[0:GEN_ROWS, :], h_bank[0:GEN_ROWS, 0:DIM], ALU.add))
                    link(v.scalar_tensor_tensor(before_relu[:], k.bn[0:GEN_ROWS, :], sum_rows[:, DIM:DIM + 1], biased[:], ALU.mult, ALU.add))
                    link(v.scalar_tensor_tensor(y[:], before_relu[:], 0.0, x_rows[:], ALU.max, ALU.add))
                    link(v.bn_stats(stats[:], y[:]))
                    dve.sem_inc(zeros_set, 1)
                    v.bn_aggr(mean_var[:], stats[:]).then_inc(var_done, 1)
                    dve.wait_ge(std_done, n + 1)
                    link(v.reciprocal(rstd[:], std[:]))
                    v.tensor_scalar(result[:], y[:], mean_var[:, 0:1], rstd[:, 0:1], ALU.subtract, ALU.mult).then_inc(result_done, 1)
                    dve.wait_ge(stored, n * 16 + 16)

            only_if_needed(dve, program)

        @block.tensor
        def _(pe):
            def program(pe):
                mm = nc.tensor.matmul
                pe.wait_ge(zeros_set, 2)
                with pe.Fori(0, GEN_STEPS, 1) as s:
                    pe.wait_ge(same_done, s + 1)
                    pe.wait_ge(rows_landed, s * 16 + 16)
                    mm(totals_bank[0:GEN_EDGES, 0:ROW], same[:], rows[:], start=True, stop=True).then_inc(totals_done, 1)
                with pe.Fori(0, GEN_TILES, 1) as n:
                    pe.wait_ge(tile_landed, n * 32 + 32)
                    nc.tensor.transpose(turn_bank[:, 0:GEN_ROWS], x_rows[:], k.identity[0:GEN_ROWS, 0:GEN_ROWS])
                    nc.tensor.transpose(turn_bank[:, GEN_ROWS:2 * GEN_ROWS], sum_rows[:, 0:DIM],
                                        k.identity[0:GEN_ROWS, 0:GEN_ROWS]).then_inc(turned, 1)
                    pe.wait_ge(turned_copied, n + 1)
                    mm(h_bank[0:GEN_ROWS, 0:DIM], x_turned[:, 0, :], k.ws_t[:], start=True, stop=False)
                    mm(h_bank[0:GEN_ROWS, 0:DIM], x_turned[:, 1, :], k.wn_t[:], start=False, stop=True).then_inc(h_done, 1)

            only_if_needed(pe, program)

        @block.scalar
        def _(act):
            def program(act):
                with act.Fori(0, GEN_TILES, 1) as n:
                    act.wait_ge(turned, n + 1)
                    nc.scalar.copy(x_turned[:], turn_bank[:, 0:2 * GEN_ROWS].rearrange("p (a r) -> p a r", a=2)).then_inc(turned_copied, 1)
                    act.wait_ge(var_done, n + 1)
                    nc.scalar.activation(std[:], mean_var[:, 1:2], ACT.Sqrt, bias=k.eps[0:GEN_ROWS, 0:1], scale=1.0).then_inc(std_done, 1)
                    act.wait_ge(result_done, n + 1)
                    act.dma_start(out[bass.ds(n * GEN_ROWS, GEN_ROWS), :], result[:]).then_inc(stored, 16)
                act.wait_ge(stored, GEN_TILES * 16)

            only_if_needed(act, program)


INPUTS = ["x", "src", "dst", "L0_gnn_W_self", "L0_gnn_b_self", "L0_gnn_W_neigh", "L0_gnn_b_neigh"]


def kernel(**inputs):
    import concourse.bacc as bacc
    from concourse.bass_utils import run_bass_kernel_spmd

    nc = bacc.Bacc("TRN2", target_bir_lowering=False, num_devices=1)
    arrays, args = {}, []
    for name in INPUTS:
        a = np.ascontiguousarray(inputs[name])
        arrays[f"in_{name}"] = a
        args.append(nc.dram_tensor(f"in_{name}", a.shape, mybir.dt.from_np(a.dtype), kind="ExternalInput").ap())
    out = nc.dram_tensor("out", (NODES, DIM), FP32, kind="ExternalOutput").ap()
    gnn_kernel(nc, *args, out)
    done = run_bass_kernel_spmd(nc, [arrays], core_ids=[0])
    return done.results[0]["out"]
```
